# Optimizing a Trainium2 kernel written in Bass

```python
import numpy as np
import jax
import jax.numpy as jnp

def _softmax(x, axis=-1):
    return jax.nn.softmax(x, axis=axis)
def _gelu(x):
    return jax.nn.gelu(x, approximate=True)
def _silu(x):
    return jax.nn.silu(x)
def _sigmoid(x):
    return jax.nn.sigmoid(x)
def _layernorm(x, axis=-1, eps=1e-5):
    m = jnp.mean(x, axis=axis, keepdims=True)
    v = jnp.var(x, axis=axis, keepdims=True)
    return (x - m) / jnp.sqrt(v + eps)
def _scatter_add(tgt, idx, src, axis=0):
    return tgt.at[idx].add(src)
def _segment_sum(src, seg, n):
    return jax.ops.segment_sum(src, seg, n)

kernel_name = 'mk_adj_resnorm_d4_adj_128_875174'

def setup_inputs(seed: int = 0):
    np.random.seed(seed)
    _w = jnp.asarray
    def _rec_inputs():
        import jax
        import jax.numpy as jnp
        _gk = jax.random.key(seed)
        x = -0.000929 + 1 * jax.random.normal(jax.random.fold_in(_gk, 1), (8192, 128), jnp.float32)
        _a = jax.random.bernoulli(jax.random.fold_in(_gk, 2), 0.000976562, (8192, 8192))
        _a = jnp.logical_or(_a, jnp.eye(8192, dtype=bool))
        _af = _a.astype(jnp.float32)
        _af = _af * jax.random.uniform(jax.random.fold_in(_gk, 3), (8192, 8192), jnp.float32, 0.05, 1)
        adj = _af
        return x, adj
    x, adj = _rec_inputs()
    def _L0_gnn_setup():
        import jax, jax.numpy as jnp
        import numpy as np
        N = 8192
        H = 128
        key = jax.random.key(seed)
        k_x, k_A, k_W = jax.random.split(key, 3)
        x = jax.random.normal(k_x, (N, H), dtype=jnp.float32)
        A = jax.random.uniform(k_A, (N, N), dtype=jnp.float32)
        alpha = jnp.array([0.5], dtype=jnp.float32)
        bound = 1.0 / np.sqrt(H)
        W = jax.random.uniform(k_W, (H, H), dtype=jnp.float32, minval=-bound, maxval=bound)
        b = jnp.zeros((H,), dtype=jnp.float32)
        t = jnp.zeros((1,), dtype=jnp.float32)
        return {'t': t, 'x': x, 'A': A, 'alpha': alpha, 'W': W, 'b': b}
    _L0_gnn_all = _L0_gnn_setup()
    _L0_gnn_in = {k: v for k, v in _L0_gnn_all.items() if k in ('t', 'alpha', 'W', 'b', )}
    del _L0_gnn_all

    def _L1_gnn_setup():
        import jax, jax.numpy as jnp
        import numpy as np
        N, E, D = (8192, 8192, 128)
        key = jax.random.key(seed)
        k1, k2 = jax.random.split(key)
        X = jax.random.normal(k1, (N, D), dtype=jnp.float32)
        H = jax.random.uniform(k2, (N, E), dtype=jnp.float32)
        return {'X': X, 'H': H}
    _L1_gnn_all = _L1_gnn_setup()
    _L1_gnn_in = {k: v for k, v in _L1_gnn_all.items() if k in ()}
    del _L1_gnn_all

    def _L2_gnn_setup():
        import jax, jax.numpy as jnp
        import numpy as np
        N_NODES = 8192
        IN_FEATURES = 128
        OUT_FEATURES = 128
        key = jax.random.key(seed)
        k_x, k_adj, k_w, k_b = jax.random.split(key, 4)
        x = jax.random.normal(k_x, (N_NODES, IN_FEATURES), dtype=jnp.float32)
        adj = jax.random.uniform(k_adj, (N_NODES, N_NODES), dtype=jnp.float32)
        bound = 1.0 / np.sqrt(IN_FEATURES)
        W = jax.random.uniform(k_w, (OUT_FEATURES, IN_FEATURES), dtype=jnp.float32, minval=-bound, maxval=bound)
        b = jax.random.uniform(k_b, (OUT_FEATURES,), dtype=jnp.float32, minval=-bound, maxval=bound)
        return {'x': x, 'adj': adj, 'W': W, 'b': b}
    _L2_gnn_all = _L2_gnn_setup()
    _L2_gnn_in = {k: v for k, v in _L2_gnn_all.items() if k in ('W', 'b', )}
    del _L2_gnn_all

    def _L3_gnn_setup():
        import jax, jax.numpy as jnp
        import numpy as np
        N = 8192
        F_IN = 128
        F_OUT = 128
        key = jax.random.key(seed)
        k1, k2, k3, k4, k5 = jax.random.split(key, 5)
        x = jax.random.normal(k1, (N, F_IN), dtype=jnp.float32)
        adj = jax.random.uniform(k2, (N, N), dtype=jnp.float32)
        kernel = jax.random.normal(k3, (F_IN, F_OUT), dtype=jnp.float32) * 0.05
        bias = jax.random.normal(k4, (F_OUT,), dtype=jnp.float32) * 0.05
        beta = jax.random.uniform(k5, (N,), dtype=jnp.float32)
        return {'x': x, 'adj': adj, 'kernel': kernel, 'bias': bias, 'beta': beta}
    _L3_gnn_all = _L3_gnn_setup()
    _L3_gnn_in = {k: v for k, v in _L3_gnn_all.items() if k in ('kernel', 'bias', 'beta', )}
    del _L3_gnn_all

    return {
        "x": x,
        "adj": adj,
        "L0_gnn_t": _L0_gnn_in["t"],
        "L0_gnn_alpha": _L0_gnn_in["alpha"],
        "L0_gnn_W": _L0_gnn_in["W"],
        "L0_gnn_b": _L0_gnn_in["b"],
        "L2_gnn_W": _L2_gnn_in["W"],
        "L2_gnn_b": _L2_gnn_in["b"],
        "L3_gnn_kernel": _L3_gnn_in["kernel"],
        "L3_gnn_bias": _L3_gnn_in["bias"],
        "L3_gnn_beta": _L3_gnn_in["beta"],
    }

def reference(x, adj, L0_gnn_t, L0_gnn_alpha, L0_gnn_W, L0_gnn_b, L2_gnn_W, L2_gnn_b, L3_gnn_kernel, L3_gnn_bias, L3_gnn_beta):
    import jax
    import jax.numpy as jnp
    def _L0_gnn_ref(t, x, A, alpha, W, b):
        import jax, jax.numpy as jnp
        import numpy as np
        N = 8192
        H = 128
        a = alpha[0]
        A_prime = a * A
        diag = jnp.diagonal(A_prime) + (1.0 - a)
        A_prime = A_prime.at[jnp.arange(N), jnp.arange(N)].set(diag)
        out_degree = A_prime.sum(axis=1)
        inv_deg = jnp.where(out_degree == 0.0, 0.0, 1.0 / out_degree)
        x = inv_deg[:, None] * A_prime @ x
        x = x @ W.T + b
        return jax.nn.relu(x)

    def _L1_gnn_ref(X, H):
        import jax, jax.numpy as jnp
        import numpy as np
        N, E, D = (8192, 8192, 128)
        msg = jnp.matmul(H.T, X)
        inv_deg = 1.0 / H.sum(axis=0)
        inv_deg = jnp.where(jnp.isinf(inv_deg), 0.0, inv_deg)
        return msg * inv_deg[:, None]

    def _L2_gnn_ref(x, adj, W, b):
        import jax, jax.numpy as jnp
        import numpy as np
        N_NODES = 8192
        IN_FEATURES = 128
        OUT_FEATURES = 128
        rowsum = adj.sum(axis=1) + 1e-08
        d_inv_sqrt = rowsum ** (-0.5)
        adj_norm = d_inv_sqrt[:, None] * adj * d_inv_sqrt[None, :]
        out = adj_norm @ x
        out = out @ W.T + b
        return out

    def _L3_gnn_ref(x, adj, kernel, bias, beta):
        import jax, jax.numpy as jnp
        import numpy as np
        N = 8192
        F_IN = 128
        F_OUT = 128
        inv_deg = 1.0 / (jnp.sum(adj, axis=1) + beta)
        agg = adj @ x + beta[:, None] * x
        out = inv_deg[:, None] * agg @ kernel + bias
        return out

    x = _layernorm(x + _L0_gnn_ref(L0_gnn_t, x, adj, L0_gnn_alpha, L0_gnn_W, L0_gnn_b), axis=-1)
    x = _layernorm(x + _L1_gnn_ref(x, adj), axis=-1)
    x = _layernorm(x + _L2_gnn_ref(x, adj, L2_gnn_W, L2_gnn_b), axis=-1)
    x = _layernorm(x + _L3_gnn_ref(x, adj, L3_gnn_kernel, L3_gnn_bias, L3_gnn_beta), axis=-1)
    return x


_drawn_inputs = setup_inputs


def setup_inputs(seed=0):
    import zlib

    import numpy as np

    out = dict(_drawn_inputs(seed))
    spreads = {'L0_gnn_b': (0.0, 0.1)}
    factors = {}
    for name, (base, spread) in spreads.items():
        noise = np.random.default_rng([zlib.crc32(name.encode()), seed]).standard_normal(out[name].shape)
        drawn = base * np.exp(spread * noise) if base else spread * noise
        out[name] = jnp.asarray(drawn.astype(out[name].dtype))
    for name, factor in factors.items():
        out[name] = (out[name] * factor).astype(out[name].dtype)
    return out
```

```python
import concourse.bass as bass
from concourse import mybir
from contextlib import ExitStack

P = 128
EPS = 1e-5


def build(nc: bass.Bass, x_in, adj, alpha, W0, b0, W2, b2, K3, b3, beta, out, x_plain):
    F32, F32R = mybir.dt.float32, mybir.dt.float32r
    ALU, ACT, AX = mybir.AluOpType, mybir.ActivationFunctionType, mybir.AxisListType

    N, F = x_in.shape
    BLOCKS = N // P
    BLOCK_ROWS = 4
    SUPER = BLOCK_ROWS * P
    SUPERS = N // SUPER
    CHUNK = 512
    GROUPS = N // CHUNK
    PER_CHUNK = CHUNK // P
    WIDE = 1024
    WIDES = N // WIDE
    RING = 4
    BANKS = 4
    LAG = 2
    HALVES = WIDE // 512
    DIAGONAL_AT = BLOCKS - 4
    FACTORS_AT = 44

    LOADS = {0: RING, 1: RING + SUPERS * GROUPS}
    LOADS[2] = LOADS[1] + WIDES * BLOCKS // 2
    LOADS[3] = LOADS[2] + SUPERS * GROUPS
    TURN = {0: 0, 2: SUPERS * BLOCKS, 3: 2 * SUPERS * BLOCKS}

    ctx = ExitStack()
    with ctx:
        def sb(name, shape, dt=F32):
            return ctx.enter_context(nc.sbuf_tensor(name, shape, dt))

        def sem(name):
            return ctx.enter_context(nc.semaphore(name))

        x_high = [sb(f"x_high{i}", [P, BLOCKS, F], F32R) for i in range(2)]
        x_low = [sb(f"x_low{i}", [P, BLOCKS, F], F32R) for i in range(2)]
        ring = sb("ring", [P, RING, BLOCK_ROWS, CHUNK])
        parts = sb("parts", [P, BANKS, 2, 512], F32R)
        acc_sb = sb("acc_sb", [P, WIDE])
        w_nat = acc_sb[:, 0:2 * F].rearrange("p (w f) -> p w f", w=2)
        beta_rows = acc_sb[0:BLOCKS, 2 * F:2 * F + P]
        x_res = sb("x_res", [P, 2, BLOCK_ROWS, F])
        u = sb("u", [P, BLOCK_ROWS, F])
        x_new = sb("x_new", [P, BLOCK_ROWS, F])
        diag = sb("diag", [P, BLOCK_ROWS, P])
        identity = sb("identity", [P, P])
        diag0 = sb("diag0", [P, P])
        w_mov = sb("w_mov", [P, 3, F])
        bias = sb("bias", [P, 3, F])
        a_bc = sb("a_bc", [P, 1])
        one_minus_a = sb("one_minus_a", [P, 1])
        beta_col = sb("beta_col", [P, BLOCKS])
        row_parts = sb("row_parts", [P, 2, GROUPS, SUPERS])
        row_acc = sb("row_acc", [P, 2, CHUNK])
        row_sum = sb("row_sum", [P, BLOCKS])
        col_parts = sb("col_parts", [P, BLOCKS, SUPERS])
        col_sum = sb("col_sum", [P, BLOCKS])
        col_factor = sb("col_factor", [P, BLOCKS])
        degree3 = sb("degree3", [P, BLOCKS])
        d_half = sb("d_half", [P, BLOCKS])
        small = row_acc[:].rearrange("p a (k b) -> p (a k) b", b=BLOCKS)
        deg = sb("deg", [P, 5, BLOCK_ROWS])
        stats = sb("stats", [P, BLOCK_ROWS, 6])
        moments = sb("moments", [P, BLOCK_ROWS, 2])
        var = sb("var", [P, BLOCK_ROWS])
        sd = sb("sd", [P, BLOCK_ROWS])
        rs = sb("rs", [P, BLOCK_ROWS])
        rt = sb("rt", [P, 4, BLOCK_ROWS])

        psum = ctx.enter_context(nc.psum_tensor("psum", [P, 8, 512], F32))
        ACC, Y, JUNK = 4, 5, 6

        arrived = [sem(f"arrived{i}") for i in range(RING)]
        const_in = sem("const_in")
        made = sem("made")
        setup_pe = sem("setup_pe")
        setup_dve = sem("setup_dve")
        x0_high_ready = sem("x0_high_ready")
        x0_ready = sem("x0_ready")
        transposed = sem("transposed")
        high_ready = sem("high_ready")
        low_ready = sem("low_ready")
        products = sem("products")
        acc_copied = sem("acc_copied")
        y_ready = sem("y_ready")
        y_used = sem("y_used")
        res_in = [sem("res_in0"), sem("res_in1")]
        res_used = sem("res_used")
        diag_ready = sem("diag_ready")
        wide_high = sem("wide_high")
        wide_low = sem("wide_low")
        wide_products = sem("wide_products")
        wide_copied = sem("wide_copied")
        rows_act = sem("rows_act")
        rows_dve = sem("rows_dve")
        rows_pool = sem("rows_pool")
        rows_done = sem("rows_done")
        deg_steps = sem("deg_steps")
        stats_ready = sem("stats_ready")
        moments_ready = sem("moments_ready")
        var_ready = sem("var_ready")
        sd_ready = sem("sd_ready")
        root_steps = sem("root_steps")
        new_ready = sem("new_ready")
        scaled_ready = sem("scaled_ready")
        split_high = sem("split_high")
        split_done = sem("split_done")
        stored = sem("stored")
        factors = sem("factors")
        factor_root = sem("factor_root")

        DEG_STEPS, ROOT_STEPS = 6, 5

        def unit(layer, t):
            return layer * SUPERS + t

        def turned(layer, s):
            return TURN[layer] // BLOCKS + s

        def slot_count(layer, g, per, s):
            return (s * (per // RING) + (LOADS[layer] + g) // RING + 1) * 16

        def res_value(layer, pair, parity):
            before = {0: 0, 1: SUPERS * (1 - parity), 2: SUPERS * 3 // 2, 3: SUPERS * 5 // 2}[layer]
            return (before + pair + 1) * 16

        (DEGREE, DEGREE2, SCALE, RESIDUAL, STATS, MOMENTS, VARIANCE, ROOT, ROOT2, NORM, TIMES_D,
         LOW) = range(12)

        def stage_at(start, spacing, block):
            stage, rest = divmod(block - start, spacing)
            return stage if rest == 0 and 0 <= stage <= LOW else None

        ALONE, PAIR_ROWS, PAIR_WIDE = (8, 2), ((4, 1), (20, 1)), ((4, 2), (34, 2))

        def stages(block, pending, wide):
            if pending is None:
                return
            layer, t, pair = pending
            if layer != 1:
                stage = stage_at(*ALONE, block)
                if stage is not None:
                    yield layer, t, 0, t, stage
                return
            for parity in range(2):
                stage = stage_at(*(PAIR_WIDE if wide else PAIR_ROWS)[parity], block)
                if stage is not None:
                    yield layer, t + parity, parity, pair, stage

        adj_chunks = adj.rearrange("(s r p) c -> s p r c", r=BLOCK_ROWS, p=P)
        adj_wides = adj.rearrange("(k r p) (q c) -> k q p r c", r=2, p=P, c=WIDE)
        x_in_quarters = x_in.rearrange("(q b p) f -> q p b f", q=RING, p=P)
        x_units = [x.rearrange("(t b p) f -> t p b f", b=BLOCK_ROWS, p=P) for x in (x_in, *x_plain, out)]

        block = ctx.enter_context(nc.Block())

        @block.sync
        def _(sp):
            def store(layer, t):
                sp.wait_ge(new_ready, unit(layer, t) + 1)
                sp.dma_start(x_units[layer + 1][t], x_new[:]).then_inc(stored, 16)

            def superblock(layer, s, pending):
                start = isinstance(s, int)
                for g in range(GROUPS):
                    n = LOADS[layer] + g
                    if start and g < RING and layer == 0:
                        sp.wait_ge(x0_ready, g + 1)
                    elif start and g < RING and layer == 2:
                        sp.wait_ge(wide_low, WIDES * BLOCKS - 2 * (RING - g - 1))
                    else:
                        loads_before = s * GROUPS + g - RING + 1
                        if layer == 0:
                            sp.wait_ge(rows_dve, loads_before)
                        else:
                            sp.wait_ge(transposed, TURN[layer] + loads_before * PER_CHUNK)
                    sp.dma_start(ring[:, n % RING], adj_chunks[s, :, :, g * CHUNK:(g + 1) * CHUNK])\
                        .then_inc(arrived[n % RING], 16)
                    if g == 8 and pending and pending[0] == 1:
                        store(1, SUPERS - 2)
                    if g == 13:
                        if pending:
                            layer_before, t, _ = pending
                            store(layer_before, SUPERS - 1 if layer_before == 1 else t)
                        if layer >= 2 and start:
                            sp.wait_ge(stored, 16 * unit(layer, 0))
                            if layer == 2:
                                sp.wait_ge(y_used, unit(2, 0))
                        if layer != 0 or not start:
                            sp.wait_ge(res_used, turned(layer, s))
                        sp.dma_start(x_res[:, 0], x_units[layer][s]).then_inc(res_in[0], 16)

            def wide_load(q, k):
                n = LOADS[1] + k
                if isinstance(q, int) and k < RING:
                    last = SUPERS * GROUPS - RING + k + 1
                    sp.wait_ge(rows_dve, last)
                else:
                    sp.wait_ge(wide_low, q * BLOCKS + 2 * (k - RING + 1))
                sp.dma_start(ring[:, n % RING].rearrange("p r c -> p (r c)").rearrange("p (r c) -> p r c", r=2),
                             adj_wides[k, q]).then_inc(arrived[n % RING], 16)

            def load_pair(q):
                for parity in range(2):
                    if isinstance(q, int):
                        sp.wait_ge(res_used, SUPERS)
                    else:
                        sp.wait_ge(y_used, unit(1, 2 * q - 1 + parity))
                    sp.dma_start(x_res[:, parity], x_units[1][2 * q + parity]).then_inc(res_in[parity], 16)

            for q in range(RING):
                sp.dma_start(ring[:, q].rearrange("p r c -> p (r c)").rearrange("p (b f) -> p b f", f=F),
                             x_in_quarters[q]).then_inc(arrived[q], 16)
            for to, of in ((a_bc[:], alpha.partition_broadcast(P)), (bias[:, 0], b0.partition_broadcast(P)),
                           (bias[:, 1], b2.partition_broadcast(P)), (bias[:, 2], b3.partition_broadcast(P)),
                           (w_nat[:, 0], W0), (w_nat[:, 1], W2), (w_mov[:, 2], K3),
                           (beta_rows, beta.rearrange("(b p) -> b p", p=P))):
                sp.dma_start(to, of).then_inc(const_in, 16)

            superblock(0, 0, None)
            with sp.Fori(1, SUPERS) as s:
                superblock(0, s, (0, s - 1, None))
            for k in range(BLOCKS // 2):
                wide_load(0, k)
                if k == 24:
                    store(0, SUPERS - 1)
                    sp.wait_ge(stored, 16 * SUPERS)
                    load_pair(0)
            with sp.Fori(1, WIDES) as q:
                for k in range(BLOCKS // 2):
                    wide_load(q, k)
                    if k == 20:
                        store(1, 2 * q - 2)
                store(1, 2 * q - 1)
                load_pair(q)
            superblock(2, 0, (1, SUPERS - 2, None))
            with sp.Fori(1, SUPERS) as s:
                superblock(2, s, (2, s - 1, None))
            superblock(3, 0, (2, SUPERS - 1, None))
            with sp.Fori(1, SUPERS) as s:
                superblock(3, s, (3, s - 1, None))
            store(3, SUPERS - 1)
            sp.wait_ge(stored, 16 * 4 * SUPERS)

        @block.tensor
        def _(pe):
            def turn(layer, s, c):
                g = c // PER_CHUNK
                n = LOADS[layer] + g
                if c % PER_CHUNK == 0:
                    pe.wait_ge(arrived[n % RING], slot_count(layer, g, GROUPS, s))
                if layer == 2 and c == 0 and isinstance(s, int):
                    pe.wait_ge(wide_copied, WIDES)
                if TURN[layer] + c >= BANKS or not isinstance(s, int):
                    pe.wait_ge(low_ready, TURN[layer] + s * BLOCKS + c - BANKS + 1)
                at = (c % PER_CHUNK) * P
                for r in range(BLOCK_ROWS):
                    last = nc.tensor.transpose(psum[:, c % BANKS, r * P:(r + 1) * P],
                                               ring[:, n % RING, r, at:at + P], identity[:])
                last.then_inc(transposed, 1)

            def multiply(layer, s, c):
                high, low, i = x_high[layer % 2], x_low[layer % 2], c % BANKS
                if c == 0 and not (layer == 0 and isinstance(s, int)):
                    pe.wait_ge(acc_copied, turned(layer, s))
                if isinstance(s, int) and s == 0:
                    if layer == 0 and c % (BLOCKS // RING) == 0:
                        pe.wait_ge(x0_ready, c // (BLOCKS // RING) + 1)
                    if layer != 0 and c % BLOCK_ROWS == 0:
                        pe.wait_ge(split_done, unit(layer - 1, c // BLOCK_ROWS) + 1)
                pe.wait_ge(low_ready, TURN[layer] + s * BLOCKS + c + 1)
                if c == DIAGONAL_AT and layer != 2:
                    pe.wait_ge(res_in[0], res_value(layer, s, 0))
                    if layer == 3:
                        pe.wait_ge(diag_ready, s + 1)
                    for r in range(BLOCK_ROWS):
                        nc.tensor.matmul(psum[:, ACC, r * P:(r + 1) * P], x_res[:, 0, r],
                                         diag0[:] if layer == 0 else diag[:, r], start=False, stop=False,
                                         skip_group_check=True)
                nc.tensor.matmul(psum[:, ACC], high[:, c], parts[:, i, 0], start=(c == 0), stop=False)
                nc.tensor.matmul(psum[:, ACC], high[:, c], parts[:, i, 1], start=False, stop=False)
                nc.tensor.matmul(psum[:, ACC], low[:, c], parts[:, i, 0], start=False, stop=(c == BLOCKS - 1))\
                    .then_inc(products, 1)

            def project(layer, t):
                pe.wait_ge(acc_copied, turned(layer, t) + 1)
                if layer != 0 or not isinstance(t, int) or t > 0:
                    pe.wait_ge(y_used, unit(layer, t))
                for r in range(BLOCK_ROWS):
                    last = nc.tensor.matmul(psum[:, Y, r * P:(r + 1) * P], acc_sb[:, r * P:(r + 1) * P],
                                            w_mov[:, {0: 0, 2: 1, 3: 2}[layer]], start=True, stop=True)
                last.then_inc(y_ready, 1)

            def turn_back(q):
                pe.wait_ge(wide_copied, q + 1)
                for parity in range(2):
                    pe.wait_ge(y_used, unit(1, 2 * q - 1 + parity))
                    for r in range(BLOCK_ROWS):
                        at = parity * SUPER + r * P
                        last = nc.tensor.transpose(psum[:, Y + parity, r * P:(r + 1) * P],
                                                   acc_sb[:, at:at + P], identity[:])
                    last.then_inc(y_ready, 1)

            def superblock(layer, s, first, pending):
                for c in range(BLOCKS):
                    turn(layer, s, c)
                    if c >= LAG:
                        multiply(layer, s, c - LAG)
                    elif not first:
                        multiply(layer, s - 1, BLOCKS + c - LAG)
                    if c == 5 and pending:
                        if pending[0] == 1:
                            turn_back(WIDES - 1)
                        else:
                            project(*pending)

            def row_layer(layer, pending):
                superblock(layer, 0, True, pending)
                with pe.Fori(1, SUPERS) as s:
                    superblock(layer, s, False, (layer, s - 1))
                for c in range(BLOCKS - LAG, BLOCKS):
                    multiply(layer, SUPERS - 1, c)

            def wide_block(q, b):
                i, first = 2 * (b % 2), isinstance(q, int)
                if b == 0 and first:
                    pe.wait_ge(low_ready, SUPERS * BLOCKS)
                elif b == 0:
                    pe.wait_ge(wide_copied, q)
                if b % BLOCK_ROWS == 0 and first:
                    pe.wait_ge(split_done, b // BLOCK_ROWS + 1)
                pe.wait_ge(wide_low, q * BLOCKS + b + 1)
                for h in range(HALVES):
                    nc.tensor.matmul(psum[:, h], x_high[1][:, b], parts[:, i + h, 0], start=(b == 0), stop=False)
                    nc.tensor.matmul(psum[:, h], x_high[1][:, b], parts[:, i + h, 1], start=False, stop=False)
                for h in range(HALVES):
                    last = nc.tensor.matmul(psum[:, h], x_low[1][:, b], parts[:, i + h, 0], start=False,
                                            stop=(b == BLOCKS - 1))
                last.then_inc(wide_products, 1)

            pe.wait_ge(made, 2)
            pe.wait_ge(const_in, 16 * 8)
            nc.tensor.transpose(psum[:, Y, 0:P], w_nat[:, 0], identity[:])
            nc.tensor.transpose(psum[:, Y, P:2 * P], w_nat[:, 1], identity[:])
            nc.tensor.transpose(psum[:, Y, 2 * P:2 * P + BLOCKS], beta_rows, identity[0:BLOCKS, 0:BLOCKS])\
                .then_inc(setup_pe, 1)
            pe.wait_ge(setup_dve, 5)

            row_layer(0, None)
            for b in range(BLOCKS):
                wide_block(0, b)
                if b == 2:
                    project(0, SUPERS - 1)
            with pe.Fori(1, WIDES) as q:
                for b in range(BLOCKS):
                    wide_block(q, b)
                    if b == 2:
                        turn_back(q - 1)
            row_layer(2, (1, None))
            row_layer(3, (2, SUPERS - 1))
            project(3, SUPERS - 1)

        def wide_tile(n, b):
            at = (b % 2) * WIDE
            return ring[:, n % RING].rearrange("p r c -> p (r c)")[:, at:at + WIDE]\
                .rearrange("p (h c) -> p h c", h=HALVES)

        @block.scalar
        def _(act):
            def high_part(layer, s, c):
                i, n = c % BANKS, TURN[layer] + c
                act.wait_ge(transposed, n + s * BLOCKS + 1)
                if layer == 2 and isinstance(s, int) and c < BANKS:
                    act.wait_ge(wide_products, WIDES * BLOCKS)
                elif n >= BANKS or not isinstance(s, int):
                    act.wait_ge(products, n + s * BLOCKS - BANKS + 1)
                sums = {"accum_out": col_parts[:, c, bass.ds(s, 1)]} if layer == 0 else {}
                nc.scalar.activation(parts[:, i, 0], psum[:, i], ACT.Copy, **sums).then_inc(high_ready, 1)

            def row_sums(s, g):
                n = LOADS[0] + g
                act.wait_ge(arrived[n % RING], slot_count(0, g, GROUPS, s))
                if g >= 2 or not isinstance(s, int):
                    act.wait_ge(rows_act, s * GROUPS + g - 1)
                nc.scalar.activation(psum[:, JUNK + g % 2], ring[:, n % RING, 0], ACT.Copy,
                                     accum_out=row_parts[:, 0, g, bass.ds(s, 1)]).then_inc(rows_act, 1)

            def copy_acc(layer, t):
                act.wait_ge(products, TURN[layer] + (t + 1) * BLOCKS)
                if layer != 0 or not isinstance(t, int):
                    act.wait_ge(y_ready, unit(layer, t))
                nc.scalar.activation(acc_sb[:, 0:SUPER], psum[:, ACC], ACT.Copy).then_inc(acc_copied, 1)

            def root(layer, t):
                act.wait_ge(var_ready, unit(layer, t) + 1)
                nc.scalar.activation(sd[:], var[:], ACT.Sqrt).then_inc(sd_ready, 1)

            def split(layer, t):
                if layer == 1:
                    act.wait_ge(scaled_ready, t + 1)
                else:
                    act.wait_ge(new_ready, unit(layer, t) + 1)
                nc.scalar.activation(x_high[(layer + 1) % 2][:, bass.ds(t * BLOCK_ROWS, BLOCK_ROWS), :],
                                     (u if layer == 1 else x_new)[:], ACT.Copy).then_inc(split_high, 1)

            def close(block, pending, wide):
                for layer, t, _, _, stage in stages(block - 1, pending, wide):
                    if stage == VARIANCE:
                        root(layer, t)
                    if stage == TIMES_D and layer != 3:
                        split(layer, t)

            def superblock(layer, s, pending):
                for c in range(BLOCKS):
                    high_part(layer, s, c)
                    if layer == 0 and c % PER_CHUNK == 2:
                        row_sums(s, c // PER_CHUNK)
                    if c == LAG and pending and pending[0] == layer:
                        copy_acc(layer, pending[1])
                    close(c, pending, False)

            def wide_high_part(q, b):
                k, i = b // 2, 2 * (b % 2)
                n = LOADS[1] + k
                if b % 2 == 0:
                    act.wait_ge(arrived[n % RING], slot_count(1, k, BLOCKS // 2, q))
                if b < 2 and isinstance(q, int):
                    act.wait_ge(products, SUPERS * BLOCKS)
                else:
                    act.wait_ge(wide_products, q * BLOCKS + b - 1)
                nc.scalar.activation(parts[:, i:i + 2, 0], wide_tile(n, b), ACT.Copy).then_inc(wide_high, 1)

            def copy_wide(q):
                act.wait_ge(wide_products, (q + 1) * BLOCKS)
                act.wait_ge(y_ready, unit(1, 2 * q))
                for h in range(HALVES):
                    last = nc.scalar.activation(acc_sb[:, h * 512:(h + 1) * 512], psum[:, h], ACT.Copy)
                last.then_inc(wide_copied, 1)

            act.wait_ge(const_in, 16 * 8)
            for q in range(RING):
                act.wait_ge(arrived[q], 16)
                to = x_high[0][:, q * (BLOCKS // RING):(q + 1) * (BLOCKS // RING)].rearrange("p b f -> p (b f)")
                nc.scalar.activation(to, ring[:, q].rearrange("p r c -> p (r c)"), ACT.Identity, scale=a_bc[:])\
                    .then_inc(x0_high_ready, 1)

            superblock(0, 0, None)
            with act.Fori(1, SUPERS) as s:
                superblock(0, s, (0, s - 1, None))
            copy_acc(0, SUPERS - 1)
            for b in range(BLOCKS):
                wide_high_part(0, b)
                close(b, (0, SUPERS - 1, None), True)
                if b == FACTORS_AT + 2:
                    act.wait_ge(factors, 7)
                    nc.scalar.activation(small[:, 1], small[:, 0], ACT.Sqrt).then_inc(factor_root, 1)
            with act.Fori(1, WIDES) as q:
                for b in range(BLOCKS):
                    wide_high_part(q, b)
                    if b == 0:
                        copy_wide(q - 1)
                    close(b, (1, 2 * q - 2, None), True)
            copy_wide(WIDES - 1)
            superblock(2, 0, (1, SUPERS - 2, None))
            with act.Fori(1, SUPERS) as s:
                superblock(2, s, (2, s - 1, None))
            copy_acc(2, SUPERS - 1)
            superblock(3, 0, (2, SUPERS - 1, None))
            with act.Fori(1, SUPERS) as s:
                superblock(3, s, (3, s - 1, None))
            copy_acc(3, SUPERS - 1)
            root(3, SUPERS - 1)

        @block.vector
        def _(dve):
            def low_part(layer, s, c):
                i = c % BANKS
                dve.wait_ge(high_ready, TURN[layer] + s * BLOCKS + c + 1)
                nc.vector.tensor_tensor(parts[:, i, 1], psum[:, i], parts[:, i, 0].bitcast(F32), ALU.subtract)\
                    .then_inc(low_ready, 1)

            def row_sums(s, g):
                n = LOADS[0] + g
                dve.wait_ge(arrived[n % RING], slot_count(0, g, GROUPS, s))
                dve.wait_ge(rows_act, s * GROUPS + g + 1)
                dve.wait_ge(rows_pool, s * (GROUPS - 1) + max(g, 1))
                nc.vector.tensor_reduce(row_parts[:, 1, g, bass.ds(s, 1)], ring[:, n % RING, 1], AX.X, ALU.add)\
                    .then_inc(rows_dve, 1)

            def rows(tensor, t):
                return tensor[:, bass.ds(t * BLOCK_ROWS, BLOCK_ROWS)]

            def unit_row_sums(t):
                dve.wait_ge(rows_act, (t + 1) * GROUPS)
                dve.wait_ge(rows_dve, (t + 1) * GROUPS)
                nc.vector.tensor_reduce(row_sum[:, bass.ds(t * BLOCK_ROWS, 2)],
                                        row_parts[:, :, :, bass.ds(t, 1)].rearrange("p r g a -> p r (g a)"),
                                        AX.X, ALU.add)
                dve.wait_ge(rows_pool, (t + 1) * (GROUPS - 1))
                nc.vector.tensor_reduce(row_sum[:, bass.ds(t * BLOCK_ROWS + 2, 2)], row_acc[:], AX.X, ALU.add)\
                    .then_inc(rows_done, 1)

            def degree(t, second):
                def after(k):
                    dve.wait_ge(deg_steps, t * DEG_STEPS + k)

                if not second:
                    dve.wait_ge(rows_done, t + 1)
                    nc.vector.tensor_scalar(deg[:, 0], rows(row_sum, t), a_bc[:], one_minus_a[:], ALU.mult, ALU.add)\
                        .then_inc(deg_steps, 1)
                    after(1)
                    nc.vector.tensor_scalar(deg[:, 1], deg[:, 0], 0.0, None, ALU.is_equal).then_inc(deg_steps, 1)
                    after(2)
                    nc.vector.tensor_tensor(deg[:, 2], deg[:, 0], deg[:, 1], ALU.add).then_inc(deg_steps, 1)
                    return
                after(3)
                nc.vector.reciprocal(deg[:, 0], deg[:, 2]).then_inc(deg_steps, 1)
                nc.vector.tensor_scalar(deg[:, 4], deg[:, 1], -1.0, 1.0, ALU.mult, ALU.add).then_inc(deg_steps, 1)
                after(5)
                nc.vector.tensor_tensor(deg[:, 3], deg[:, 0], deg[:, 4], ALU.mult).then_inc(deg_steps, 1)

            def scale(layer, t, parity, pair):
                dve.wait_ge(y_ready, unit(layer, t) + 1)
                if layer == 0:
                    dve.wait_ge(deg_steps, (t + 1) * DEG_STEPS)
                    by = deg[:, 3]
                elif layer == 2:
                    by = rows(d_half, t)
                    if isinstance(t, int) and t == 0:
                        dve.wait_ge(split_done, unit(2, 0))
                else:
                    by = rows(col_factor if layer == 1 else degree3, t)
                if layer == 1:
                    dve.wait_ge(res_in[parity], res_value(1, pair, parity))
                    dve.wait_ge(split_done, unit(1, t))
                for r in range(BLOCK_ROWS):
                    plus = x_res[:, parity, r] if layer == 1 else bias[:, {0: 0, 2: 1, 3: 2}[layer]]
                    last = nc.vector.scalar_tensor_tensor(u[:, r], psum[:, Y + parity, r * P:(r + 1) * P],
                                                          by[:, r:r + 1], plus, ALU.mult, ALU.add)
                last.then_inc(y_used, 1)

            def residual(layer, t):
                dve.wait_ge(y_used, unit(layer, t) + 1)
                dve.wait_ge(res_in[0], res_value(layer, t, 0))
                if layer == 0:
                    done = nc.vector.scalar_tensor_tensor(u[:], u[:], 0.0, x_res[:, 0], ALU.max, ALU.add)
                else:
                    done = nc.vector.tensor_tensor(u[:], u[:], x_res[:, 0], ALU.add)
                done.then_inc(res_used, 1)

            def close(block, pending, wide):
                for layer, t, parity, pair, stage in stages(block, pending, wide):
                    close_stage(layer, t, parity, pair, stage)

            def close_stage(layer, t, parity, pair, stage):
                    n = unit(layer, t)
                    if stage == DEGREE and layer == 0:
                        degree(t, False)
                    if stage == DEGREE2 and layer == 0:
                        degree(t, True)
                    if stage == SCALE:
                        scale(layer, t, parity, pair)
                    if stage == RESIDUAL and layer != 1:
                        residual(layer, t)
                    if stage == STATS:
                        if layer == 1:
                            dve.wait_ge(y_used, n + 1)
                        else:
                            dve.wait_ge(res_used, turned(layer, t) + 1)
                        for r in range(BLOCK_ROWS):
                            last = nc.vector.bn_stats(stats[:, r], u[:, r])
                        last.then_inc(stats_ready, 1)
                    if stage == MOMENTS:
                        dve.wait_ge(stats_ready, n + 1)
                        nc.vector.tensor_copy(rt[:, 0], stats[:, :, 0])
                        for r in range(BLOCK_ROWS):
                            last = nc.vector.bn_aggr(moments[:, r], stats[:, r])
                        last.then_inc(moments_ready, 1)
                    if stage == VARIANCE:
                        dve.wait_ge(moments_ready, n + 1)
                        nc.vector.tensor_scalar(var[:], moments[:, :, 1], EPS, None, ALU.add).then_inc(var_ready, 1)
                    if stage == ROOT:
                        dve.wait_ge(sd_ready, n + 1)
                        nc.vector.reciprocal(rs[:], sd[:]).then_inc(root_steps, 1)
                        dve.wait_ge(root_steps, n * ROOT_STEPS + 1)
                        nc.vector.tensor_tensor(rt[:, 0], var[:], rs[:], ALU.mult).then_inc(root_steps, 1)
                        dve.wait_ge(root_steps, n * ROOT_STEPS + 2)
                        nc.vector.tensor_tensor(rt[:, 1], rt[:, 0], rs[:], ALU.mult).then_inc(root_steps, 1)
                    if stage == ROOT2:
                        dve.wait_ge(root_steps, n * ROOT_STEPS + 3)
                        nc.vector.tensor_scalar(rt[:, 2], rt[:, 1], -0.5, 1.5, ALU.mult, ALU.add)\
                            .then_inc(root_steps, 1)
                        dve.wait_ge(root_steps, n * ROOT_STEPS + 4)
                        nc.vector.tensor_tensor(rt[:, 3], rt[:, 2], rs[:], ALU.mult).then_inc(root_steps, 1)
                    if stage == NORM:
                        dve.wait_ge(root_steps, (n + 1) * ROOT_STEPS)
                        if not (layer == 0 and isinstance(t, int) and t == 0):
                            dve.wait_ge(stored, 16 * n)
                            dve.wait_ge(split_done, min_split(layer, t))
                        for r in range(BLOCK_ROWS):
                            last = nc.vector.tensor_scalar(x_new[:, r], u[:, r], moments[:, r, 0:1],
                                                           rt[:, 3, r:r + 1], ALU.subtract, ALU.mult)
                        last.then_inc(new_ready, 1)
                    if stage == TIMES_D and layer == 1:
                        dve.wait_ge(new_ready, n + 1)
                        by = rows(d_half, t)
                        for r in range(BLOCK_ROWS):
                            last = nc.vector.tensor_scalar(u[:, r], x_new[:, r], by[:, r:r + 1], None,
                                                           ALU.mult)
                        last.then_inc(scaled_ready, 1)
                    if stage == LOW and layer != 3:
                        dve.wait_ge(split_high, n + 1)
                        span = bass.ds(t * BLOCK_ROWS, BLOCK_ROWS)
                        nc.vector.tensor_tensor(x_low[(layer + 1) % 2][:, span, :],
                                                (u if layer == 1 else x_new)[:],
                                                x_high[(layer + 1) % 2][:, span, :].bitcast(F32), ALU.subtract)\
                            .then_inc(split_done, 1)

            def min_split(layer, t):
                return unit(3, 0) if layer == 3 else unit(layer, t)

            def diagonal(s):
                dve.wait_ge(products, TURN[3] + s * BLOCKS)
                for r in range(BLOCK_ROWS):
                    last = nc.vector.tensor_scalar(diag[:, r], identity[:],
                                                   rows(beta_col, s)[:, r:r + 1], None, ALU.mult)
                last.then_inc(diag_ready, 1)

            def superblock(layer, s, pending):
                for c in range(BLOCKS):
                    if c == 0 and layer == 0 and pending:
                        unit_row_sums(pending[1])
                    low_part(layer, s, c)
                    if layer == 0 and c % PER_CHUNK == PER_CHUNK - 1:
                        row_sums(s, c // PER_CHUNK)
                    if layer == 3 and c == 40:
                        diagonal(s)
                    close(c, pending, False)

            def wide_low_part(q, b):
                i, n = 2 * (b % 2), LOADS[1] + b // 2
                dve.wait_ge(wide_high, q * BLOCKS + b + 1)
                nc.vector.tensor_tensor(parts[:, i:i + 2, 1], wide_tile(n, b), parts[:, i:i + 2, 0].bitcast(F32),
                                        ALU.subtract).then_inc(wide_low, 1)

            def layer_factors(part):
                def after(k):
                    dve.wait_ge(factors, k)

                if part == 0:
                    nc.vector.tensor_reduce(col_sum[:], col_parts[:], AX.X, ALU.add).then_inc(factors, 1)
                    after(1)
                    nc.vector.tensor_scalar(small[:, 2], col_sum[:], 0.0, None, ALU.is_equal).then_inc(factors, 1)
                    after(2)
                    nc.vector.tensor_tensor(small[:, 3], col_sum[:], small[:, 2], ALU.add).then_inc(factors, 1)
                    after(3)
                    nc.vector.reciprocal(small[:, 4], small[:, 3]).then_inc(factors, 1)
                    nc.vector.tensor_scalar(small[:, 5], small[:, 2], -1.0, 1.0, ALU.mult, ALU.add)\
                        .then_inc(factors, 1)
                    after(5)
                    nc.vector.tensor_tensor(col_factor[:], small[:, 4], small[:, 5], ALU.mult).then_inc(factors, 1)
                    nc.vector.tensor_scalar(small[:, 0], row_sum[:], 1e-8, None, ALU.add).then_inc(factors, 1)
                if part == 1:
                    nc.vector.tensor_tensor(small[:, 6], row_sum[:], beta_col[:], ALU.add).then_inc(factors, 1)
                    after(8)
                    nc.vector.reciprocal(degree3[:], small[:, 6]).then_inc(factors, 1)
                    dve.wait_ge(factor_root, 1)
                    nc.vector.reciprocal(small[:, 7], small[:, 1]).then_inc(factors, 1)
                    after(10)
                    nc.vector.tensor_tensor(small[:, 8], small[:, 0], small[:, 7], ALU.mult).then_inc(factors, 1)
                    after(11)
                    nc.vector.tensor_tensor(small[:, 9], small[:, 8], small[:, 7], ALU.mult).then_inc(factors, 1)
                    after(12)
                    nc.vector.tensor_scalar(small[:, 10], small[:, 9], -0.5, 1.5, ALU.mult, ALU.add)\
                        .then_inc(factors, 1)
                    after(13)
                    nc.vector.tensor_tensor(d_half[:], small[:, 10], small[:, 7], ALU.mult).then_inc(factors, 1)
                    after(14)

            dve.wait_ge(const_in, 16 * 8)
            nc.vector.tensor_scalar(one_minus_a[:], a_bc[:], -1.0, 1.0, ALU.mult, ALU.add).then_inc(setup_dve, 1)
            dve.wait_ge(setup_dve, 1)
            dve.wait_ge(made, 2)
            nc.vector.tensor_scalar(diag0[:], identity[:], one_minus_a[:], None, ALU.mult).then_inc(setup_dve, 1)
            dve.wait_ge(setup_pe, 1)
            for i in range(2):
                nc.vector.tensor_copy(w_mov[:, i], psum[:, Y, i * P:(i + 1) * P]).then_inc(setup_dve, 1)
            nc.vector.tensor_copy(beta_col[:], psum[:, Y, 2 * P:2 * P + BLOCKS]).then_inc(setup_dve, 1)
            dve.wait_ge(setup_dve, 5)
            for q in range(RING):
                span = slice(q * (BLOCKS // RING), (q + 1) * (BLOCKS // RING))
                dve.wait_ge(x0_high_ready, q + 1)
                nc.vector.scalar_tensor_tensor(x_low[0][:, span].rearrange("p b f -> p (b f)"),
                                               ring[:, q].rearrange("p r c -> p (r c)"), a_bc[:],
                                               x_high[0][:, span].rearrange("p b f -> p (b f)").bitcast(F32),
                                               ALU.mult, ALU.subtract).then_inc(x0_ready, 1)

            superblock(0, 0, None)
            with dve.Fori(1, SUPERS) as s:
                superblock(0, s, (0, s - 1, None))
            for b in range(BLOCKS):
                wide_low_part(0, b)
                if b == 0:
                    unit_row_sums(SUPERS - 1)
                close(b, (0, SUPERS - 1, None), True)
                if b == FACTORS_AT:
                    layer_factors(0)
                if b == FACTORS_AT + 4:
                    layer_factors(1)
            with dve.Fori(1, WIDES) as q:
                for b in range(BLOCKS):
                    wide_low_part(q, b)
                    close(b, (1, 2 * q - 2, q - 1), True)
            superblock(2, 0, (1, SUPERS - 2, WIDES - 1))
            with dve.Fori(1, SUPERS) as s:
                superblock(2, s, (2, s - 1, None))
            superblock(3, 0, (2, SUPERS - 1, None))
            with dve.Fori(1, SUPERS) as s:
                superblock(3, s, (3, s - 1, None))
            for stage in range(LOW + 1):
                close_stage(3, SUPERS - 1, 0, None, stage)

        @block.gpsimd
        def _(pool):
            nc.gpsimd.memset(identity[:], 0.0).then_inc(made, 1)
            pool.wait_ge(made, 1)
            nc.gpsimd.affine_select(out=identity[:], in_=identity[:], compare_op=ALU.not_equal, fill=1.0, base=0,
                                    pattern=[[-1, P]], channel_multiplier=1).then_inc(made, 1)

            def row_sums(s):
                for g in range(GROUPS):
                    n = LOADS[0] + g
                    pool.wait_ge(arrived[n % RING], slot_count(0, g, GROUPS, s))
                    if g == 0:
                        continue
                    if g == 1:
                        before = ring[:, LOADS[0] % RING, 2:4]
                        if not isinstance(s, int):
                            pool.wait_ge(rows_done, s)
                    else:
                        before = row_acc[:]
                        pool.wait_ge(rows_pool, s * (GROUPS - 1) + g - 1)
                    nc.gpsimd.tensor_tensor(row_acc[:], before, ring[:, n % RING, 2:4], ALU.add)\
                        .then_inc(rows_pool, 1)

            row_sums(0)
            with pool.Fori(1, SUPERS) as s:
                row_sums(s)


_ARGS = ["x", "adj", "L0_gnn_alpha", "L0_gnn_W", "L0_gnn_b", "L2_gnn_W", "L2_gnn_b", "L3_gnn_kernel",
         "L3_gnn_bias", "L3_gnn_beta"]


def kernel(x, adj, L0_gnn_t, L0_gnn_alpha, L0_gnn_W, L0_gnn_b, L2_gnn_W, L2_gnn_b, L3_gnn_kernel,
           L3_gnn_bias, L3_gnn_beta):
    import numpy as np
    import concourse.bacc as bacc
    from concourse.bass_utils import run_bass_kernel_spmd

    given = [x, adj, L0_gnn_alpha, L0_gnn_W, L0_gnn_b, L2_gnn_W, L2_gnn_b, L3_gnn_kernel, L3_gnn_bias,
             L3_gnn_beta]
    nc = bacc.Bacc("TRN2", target_bir_lowering=False, num_devices=1)
    arrays, args = {}, []
    for name, value in zip(_ARGS, given):
        a = np.ascontiguousarray(value)
        arrays[f"in_{name}"] = a
        args.append(nc.dram_tensor(f"in_{name}", a.shape, mybir.dt.from_np(a.dtype), kind="ExternalInput").ap())
    out = nc.dram_tensor("out", x.shape, mybir.dt.float32, kind="ExternalOutput").ap()
    plain = [nc.dram_tensor(f"x{i + 1}_plain", x.shape, mybir.dt.float32, kind="Internal").ap() for i in range(3)]
    build(nc, *args, out, plain)
    return run_bass_kernel_spmd(nc, [arrays], core_ids=[0]).results[0]["out"]
```

```python
import concourse.bass as bass
from concourse import mybir
from contextlib import ExitStack

P = 128
EPS = 1e-5
KEPT_GROUPS = 8


def build(nc: bass.Bass, x_in, adj, alpha, W0, b0, W2, b2, K3, b3, beta, out, x_plain, a_turned):
    F32, F32R = mybir.dt.float32, mybir.dt.float32r
    ALU, ACT, AX = mybir.AluOpType, mybir.ActivationFunctionType, mybir.AxisListType

    N, F = x_in.shape
    BLOCKS = N // P
    BLOCK_ROWS = 4
    SUPER = BLOCK_ROWS * P
    SUPERS = N // SUPER
    CHUNK = 512
    GROUPS = N // CHUNK
    PER_CHUNK = CHUNK // P
    WIDE = 1024
    WIDES = N // WIDE
    RING = 4
    BANKS = 4
    LAG = 3
    HALVES = WIDE // 512
    WIDE_TILES = BLOCKS * HALVES
    KEPT = a_turned.shape[1]
    DIAGONAL_AT = BLOCKS - 4
    FACTORS_AT = 44

    def is_kept(g):
        return (g + 1) * KEPT // GROUPS > g * KEPT // GROUPS

    def kept_index(g):
        return g * KEPT // GROUPS

    LOADS = {0: RING, 1: RING + SUPERS * GROUPS}
    LOADS[2] = LOADS[1] + WIDES * BLOCKS // 2
    LOADS[3] = LOADS[2] + SUPERS * GROUPS
    TURN = {0: 0, 2: SUPERS * BLOCKS, 3: 2 * SUPERS * BLOCKS}

    ctx = ExitStack()
    with ctx:
        def sb(name, shape, dt=F32):
            return ctx.enter_context(nc.sbuf_tensor(name, shape, dt))

        def sem(name):
            return ctx.enter_context(nc.semaphore(name))

        x_high = [sb(f"x_high{i}", [P, BLOCKS, F], F32R) for i in range(2)]
        x_low = [sb(f"x_low{i}", [P, BLOCKS, F], F32R) for i in range(2)]
        ring = sb("ring", [P, RING, BLOCK_ROWS, CHUNK])
        parts = sb("parts", [P, BANKS, 2, 512], F32R)
        acc_sb = sb("acc_sb", [P, WIDE])
        w_nat = acc_sb[:, 0:2 * F].rearrange("p (w f) -> p w f", w=2)
        beta_rows = acc_sb[0:BLOCKS, 2 * F:2 * F + P]
        diag0 = acc_sb[:, 512:512 + P]
        x_res0 = sb("x_res0", [P, BLOCK_ROWS, F])
        kept = sb("kept", [P, BANKS, 512])
        x_new = sb("x_new", [P, BLOCK_ROWS, F])
        identity = sb("identity", [P, P])
        w_mov = sb("w_mov", [P, 3, F])
        bias = sb("bias", [P, 3, F])
        a_bc = sb("a_bc", [P, 1])
        one_minus_a = sb("one_minus_a", [P, 1])
        beta_col = sb("beta_col", [P, BLOCKS])
        row_parts = sb("row_parts", [P, 2, GROUPS, SUPERS])
        x_res = [x_res0, row_parts[:].rearrange("p a g s -> p (a g s)").rearrange("p (b f) -> p b f", f=F)]
        row_acc = sb("row_acc", [P, 2, CHUNK])
        row_sum = sb("row_sum", [P, BLOCKS])
        col_parts = sb("col_parts", [P, BLOCKS, SUPERS])
        diag = col_parts[:].rearrange("p b s -> p (b s)")[:, 0:SUPER].rearrange("p (b q) -> p b q", q=P)
        col_sum = sb("col_sum", [P, BLOCKS])
        col_factor = sb("col_factor", [P, BLOCKS])
        degree3 = sb("degree3", [P, BLOCKS])
        d_half = sb("d_half", [P, BLOCKS])
        small = row_acc[:].rearrange("p a (k b) -> p (a k) b", b=BLOCKS)
        deg = sb("deg", [P, 5, BLOCK_ROWS])
        stats = sb("stats", [P, BLOCK_ROWS, 6])
        moments = sb("moments", [P, BLOCK_ROWS, 2])
        var = sb("var", [P, BLOCK_ROWS])
        sd = sb("sd", [P, BLOCK_ROWS])
        rs = sb("rs", [P, BLOCK_ROWS])
        rt = sb("rt", [P, 4, BLOCK_ROWS])

        psum = ctx.enter_context(nc.psum_tensor("psum", [P, 8, 512], F32))
        ACC, Y = 4, 5
        u = psum[:, 7].rearrange("p (b f) -> p b f", f=F)

        arrived = [sem(f"arrived{i}") for i in range(RING)]
        const_in = sem("const_in")
        made = sem("made")
        setup_pe = sem("setup_pe")
        setup_dve = sem("setup_dve")
        x0_high_ready = sem("x0_high_ready")
        x0_ready = sem("x0_ready")
        transposed = sem("transposed")
        high_ready = sem("high_ready")
        low_ready = sem("low_ready")
        products = sem("products")
        acc_copied = sem("acc_copied")
        y_ready = sem("y_ready")
        y_used = sem("y_used")
        res_in = [sem("res_in0"), sem("res_in1")]
        res_used = sem("res_used")
        diag_ready = sem("diag_ready")
        wide_high = sem("wide_high")
        wide_low = sem("wide_low")
        wide_products = sem("wide_products")
        wide_copied = sem("wide_copied")
        kept_ready = sem("kept_ready")
        kept_out = [sem(f"kept_out{i}") for i in range(BANKS)]
        rows_dve = sem("rows_dve")
        rows_pool = sem("rows_pool")
        rows_done = sem("rows_done")
        deg_steps = sem("deg_steps")
        stats_ready = sem("stats_ready")
        moments_ready = sem("moments_ready")
        var_ready = sem("var_ready")
        sd_ready = sem("sd_ready")
        root_steps = sem("root_steps")
        new_ready = sem("new_ready")
        scaled_ready = sem("scaled_ready")
        split_high = sem("split_high")
        split_done = sem("split_done")
        stored = sem("stored")
        factors = sem("factors")
        factor_root = sem("factor_root")

        DEG_STEPS, ROOT_STEPS = 6, 5

        def loaded(layer, c):
            return layer != 0 and is_kept(c // PER_CHUNK)

        def turned_tiles(layer, s, c):
            if layer == 0:
                return s * BLOCKS + c
            g = c // PER_CHUNK
            return (SUPERS * BLOCKS + ((layer - 2) * SUPERS + s) * (GROUPS - KEPT) * PER_CHUNK
                    + (g - kept_index(g)) * PER_CHUNK + c % PER_CHUNK)

        def kept_tiles(s, g):
            return (s * KEPT + kept_index(g)) * PER_CHUNK

        def unit(layer, t):
            return layer * SUPERS + t

        def turned(layer, s):
            return TURN[layer] // BLOCKS + s

        def slot_count(layer, g, per, s):
            return (s * (per // RING) + (LOADS[layer] + g) // RING + 1) * 16

        def res_value(layer, pair, parity):
            before = {0: 0, 1: SUPERS * (1 - parity), 2: SUPERS * 3 // 2, 3: SUPERS * 5 // 2}[layer]
            return (before + pair + 1) * 16

        (DEGREE, DEGREE2, SCALE, RESIDUAL, STATS, MOMENTS, VARIANCE, ROOT, ROOT2, NORM, TIMES_D,
         LOW) = range(12)

        def stage_at(start, spacing, block):
            stage, rest = divmod(block - start, spacing)
            return stage if rest == 0 and 0 <= stage <= LOW else None

        ALONE, PAIR_ROWS, PAIR_WIDE = (8, 2), ((4, 1), (20, 1)), ((4, 2), (34, 2))

        def stages(block, pending, wide):
            if pending is None:
                return
            layer, t, pair = pending
            if layer != 1:
                stage = stage_at(*ALONE, block)
                if stage is not None:
                    yield layer, t, 0, t, stage
                return
            for parity in range(2):
                stage = stage_at(*(PAIR_WIDE if wide else PAIR_ROWS)[parity], block)
                if stage is not None:
                    yield layer, t + parity, parity, pair, stage

        adj_chunks = adj.rearrange("(s r p) c -> s p r c", r=BLOCK_ROWS, p=P)
        adj_wides = adj.rearrange("(k r p) (q c) -> k q p r c", r=2, p=P, c=WIDE)
        x_in_quarters = x_in.rearrange("(q b p) f -> q p b f", q=RING, p=P)
        x_units = [x.rearrange("(t b p) f -> t p b f", b=BLOCK_ROWS, p=P) for x in (x_in, *x_plain, out)]

        block = ctx.enter_context(nc.Block())

        @block.sync
        def _(sp):
            def store(layer, t):
                sp.wait_ge(new_ready, unit(layer, t) + 1)
                sp.dma_start(x_units[layer + 1][t], x_new[:]).then_inc(stored, 16)

            def keep(s, g):
                for k in range(PER_CHUNK):
                    sp.wait_ge(kept_ready, kept_tiles(s, g) + k + 1)
                    sp.dma_start(a_turned[s, kept_index(g), :, k, :], kept[:, k]).then_inc(kept_out[k], 16)

            def superblock(layer, s, pending):
                start = isinstance(s, int) and s == 0
                for g in range(GROUPS):
                    n = LOADS[layer] + g
                    if start and g < RING and layer == 0:
                        sp.wait_ge(x0_ready, g + 1)
                    elif start and g < RING and layer == 2:
                        sp.wait_ge(wide_low, WIDES * WIDE_TILES - 2 * HALVES * (RING - g - 1))
                    else:
                        loads_before = s * GROUPS + g - RING + 1
                        if layer == 0:
                            sp.wait_ge(rows_dve, loads_before)
                        else:
                            sp.wait_ge(low_ready, TURN[layer] + loads_before * PER_CHUNK)
                    if layer == 2 and start and is_kept(g) and kept_index(g) == 0:
                        for i in range(BANKS):
                            sp.wait_ge(kept_out[i], 16 * SUPERS * KEPT)
                    of = (a_turned[s, kept_index(g)] if layer != 0 and is_kept(g)
                          else adj_chunks[s, :, :, g * CHUNK:(g + 1) * CHUNK])
                    sp.dma_start(ring[:, n % RING], of).then_inc(arrived[n % RING], 16)
                    behind = (g - RING + 1) % GROUPS
                    if layer == 0 and is_kept(behind) and (behind <= g or not start):
                        keep(s if behind <= g else s - 1, behind)
                    if g == 8 and pending and pending[0] == 1:
                        store(1, SUPERS - 2)
                    if g == 13:
                        if pending:
                            layer_before, t, _ = pending
                            store(layer_before, SUPERS - 1 if layer_before == 1 else t)
                        if layer >= 2 and start:
                            sp.wait_ge(stored, 16 * unit(layer, 0))
                            if layer == 2:
                                sp.wait_ge(y_used, unit(2, 0))
                        if layer != 0 or not start:
                            sp.wait_ge(res_used, turned(layer, s))
                        sp.dma_start(x_res[0][:], x_units[layer][s]).then_inc(res_in[0], 16)

            def wide_load(q, k):
                n = LOADS[1] + k
                if isinstance(q, int) and k < RING:
                    last = SUPERS * GROUPS - RING + k + 1
                    sp.wait_ge(rows_dve, last)
                else:
                    sp.wait_ge(wide_low, q * WIDE_TILES + 2 * HALVES * (k - RING + 1))
                sp.dma_start(ring[:, n % RING].rearrange("p r c -> p (r c)").rearrange("p (r c) -> p r c", r=2),
                             adj_wides[k, q]).then_inc(arrived[n % RING], 16)

            def load_pair(q):
                for parity in range(2):
                    if isinstance(q, int):
                        sp.wait_ge(res_used, SUPERS)
                        sp.wait_ge(rows_done, SUPERS)
                    else:
                        sp.wait_ge(y_used, unit(1, 2 * q - 1 + parity))
                    sp.dma_start(x_res[parity][:], x_units[1][2 * q + parity]).then_inc(res_in[parity], 16)

            for q in range(RING):
                sp.dma_start(ring[:, q].rearrange("p r c -> p (r c)").rearrange("p (b f) -> p b f", f=F),
                             x_in_quarters[q]).then_inc(arrived[q], 16)
            for to, of in ((a_bc[:], alpha.partition_broadcast(P)), (bias[:, 0], b0.partition_broadcast(P)),
                           (bias[:, 1], b2.partition_broadcast(P)), (bias[:, 2], b3.partition_broadcast(P)),
                           (w_nat[:, 0], W0), (w_nat[:, 1], W2), (w_mov[:, 2], K3),
                           (beta_rows, beta.rearrange("(b p) -> b p", p=P))):
                sp.dma_start(to, of).then_inc(const_in, 16)

            superblock(0, 0, None)
            with sp.Fori(1, SUPERS) as s:
                superblock(0, s, (0, s - 1, None))
            for k in range(BLOCKS // 2):
                wide_load(0, k)
                if k < RING - 1 and is_kept(GROUPS + k - RING + 1):
                    keep(SUPERS - 1, GROUPS + k - RING + 1)
                if k == 24:
                    store(0, SUPERS - 1)
                    sp.wait_ge(stored, 16 * SUPERS)
                    load_pair(0)
            with sp.Fori(1, WIDES) as q:
                for k in range(BLOCKS // 2):
                    wide_load(q, k)
                    if k == 20:
                        store(1, 2 * q - 2)
                store(1, 2 * q - 1)
                load_pair(q)
            superblock(2, 0, (1, SUPERS - 2, None))
            with sp.Fori(1, SUPERS) as s:
                superblock(2, s, (2, s - 1, None))
            superblock(3, 0, (2, SUPERS - 1, None))
            with sp.Fori(1, SUPERS) as s:
                superblock(3, s, (3, s - 1, None))
            store(3, SUPERS - 1)
            sp.wait_ge(stored, 16 * 4 * SUPERS)

        @block.tensor
        def _(pe):
            def turn(layer, s, c):
                g = c // PER_CHUNK
                n = LOADS[layer] + g
                if c % PER_CHUNK == 0:
                    pe.wait_ge(arrived[n % RING], slot_count(layer, g, GROUPS, s))
                if layer == 2 and isinstance(s, int) and c == 0:
                    pe.wait_ge(wide_copied, WIDES)
                if TURN[layer] + c >= BANKS or not isinstance(s, int):
                    pe.wait_ge(low_ready, TURN[layer] + s * BLOCKS + c - BANKS + 1)
                at = (c % PER_CHUNK) * P
                for r in range(BLOCK_ROWS):
                    last = nc.tensor.transpose(psum[:, c % BANKS, r * P:(r + 1) * P],
                                               ring[:, n % RING, r, at:at + P], identity[:])
                last.then_inc(transposed, 1)

            def multiply(layer, s, c):
                high, low, i = x_high[layer % 2], x_low[layer % 2], c % BANKS
                if c == 0 and not (layer == 0 and isinstance(s, int)):
                    pe.wait_ge(acc_copied, turned(layer, s))
                if isinstance(s, int) and s == 0:
                    if layer == 0 and c % (BLOCKS // RING) == 0:
                        pe.wait_ge(x0_ready, c // (BLOCKS // RING) + 1)
                    if layer != 0 and c % BLOCK_ROWS == 0:
                        pe.wait_ge(split_done, unit(layer - 1, c // BLOCK_ROWS) + 1)
                pe.wait_ge(low_ready, TURN[layer] + s * BLOCKS + c + 1)
                if c == DIAGONAL_AT and layer != 2:
                    pe.wait_ge(res_in[0], res_value(layer, s, 0))
                    if layer == 3:
                        pe.wait_ge(diag_ready, s + 1)
                    for r in range(BLOCK_ROWS):
                        nc.tensor.matmul(psum[:, ACC, r * P:(r + 1) * P], x_res[0][:, r],
                                         diag0[:] if layer == 0 else diag[:, r], start=False, stop=False,
                                         skip_group_check=True)
                nc.tensor.matmul(psum[:, ACC], high[:, c], parts[:, i, 0], start=(c == 0), stop=False)
                nc.tensor.matmul(psum[:, ACC], high[:, c], parts[:, i, 1], start=False, stop=False)
                nc.tensor.matmul(psum[:, ACC], low[:, c], parts[:, i, 0], start=False, stop=(c == BLOCKS - 1))\
                    .then_inc(products, 1)

            def project(layer, t):
                pe.wait_ge(acc_copied, turned(layer, t) + 1)
                if layer != 0 or not isinstance(t, int) or t > 0:
                    pe.wait_ge(y_used, unit(layer, t))
                for r in range(BLOCK_ROWS):
                    last = nc.tensor.matmul(psum[:, Y, r * P:(r + 1) * P], acc_sb[:, r * P:(r + 1) * P],
                                            w_mov[:, {0: 0, 2: 1, 3: 2}[layer]], start=True, stop=True)
                last.then_inc(y_ready, 1)

            def turn_back(q):
                pe.wait_ge(wide_copied, q + 1)
                for parity in range(2):
                    pe.wait_ge(y_used, unit(1, 2 * q - 1 + parity))
                    for r in range(BLOCK_ROWS):
                        at = parity * SUPER + r * P
                        last = nc.tensor.transpose(psum[:, Y + parity, r * P:(r + 1) * P],
                                                   acc_sb[:, at:at + P], identity[:])
                    last.then_inc(y_ready, 1)

            def superblock(layer, s, first, pending):
                for c in range(BLOCKS):
                    if not loaded(layer, c):
                        turn(layer, s, c)
                    if c >= LAG:
                        multiply(layer, s, c - LAG)
                    elif not first:
                        multiply(layer, s - 1, BLOCKS + c - LAG)
                    if c == 5 and pending:
                        if pending[0] == 1:
                            turn_back(WIDES - 1)
                        else:
                            project(*pending)

            def row_layer(layer, pending):
                superblock(layer, 0, True, pending)
                with pe.Fori(1, SUPERS) as s:
                    superblock(layer, s, False, (layer, s - 1))
                for c in range(BLOCKS - LAG, BLOCKS):
                    multiply(layer, SUPERS - 1, c)

            def wide_block(q, b):
                first = isinstance(q, int)
                if b == 0 and first:
                    pe.wait_ge(low_ready, SUPERS * BLOCKS)
                elif b == 0:
                    pe.wait_ge(wide_copied, q)
                if b % BLOCK_ROWS == 0 and first:
                    pe.wait_ge(split_done, b // BLOCK_ROWS + 1)
                for h in range(HALVES):
                    i = (b * HALVES + h) % BANKS
                    pe.wait_ge(wide_low, q * WIDE_TILES + b * HALVES + h + 1)
                    nc.tensor.matmul(psum[:, h], x_high[1][:, b], parts[:, i, 0], start=(b == 0), stop=False)
                    nc.tensor.matmul(psum[:, h], x_high[1][:, b], parts[:, i, 1], start=False, stop=False)
                    nc.tensor.matmul(psum[:, h], x_low[1][:, b], parts[:, i, 0], start=False,
                                     stop=(b == BLOCKS - 1)).then_inc(wide_products, 1)

            pe.wait_ge(made, 2)
            pe.wait_ge(const_in, 16 * 8)
            nc.tensor.transpose(psum[:, Y, 0:P], w_nat[:, 0], identity[:])
            nc.tensor.transpose(psum[:, Y, P:2 * P], w_nat[:, 1], identity[:])
            nc.tensor.transpose(psum[:, Y, 2 * P:2 * P + BLOCKS], beta_rows, identity[0:BLOCKS, 0:BLOCKS])\
                .then_inc(setup_pe, 1)
            pe.wait_ge(setup_dve, 5)

            row_layer(0, None)
            for b in range(BLOCKS):
                wide_block(0, b)
                if b == 2:
                    project(0, SUPERS - 1)
            with pe.Fori(1, WIDES) as q:
                for b in range(BLOCKS):
                    wide_block(q, b)
                    if b == 2:
                        turn_back(q - 1)
            row_layer(2, (1, None))
            row_layer(3, (2, SUPERS - 1))
            project(3, SUPERS - 1)

        def wide_tile(n, b, h):
            at = (b % 2) * WIDE + h * 512
            return ring[:, n % RING].rearrange("p r c -> p (r c)")[:, at:at + 512]

        @block.scalar
        def _(act):
            def high_part(layer, s, c):
                i, n = c % BANKS, TURN[layer] + c
                g = c // PER_CHUNK
                if loaded(layer, c):
                    if c % PER_CHUNK == 0:
                        slot = (LOADS[layer] + g) % RING
                        act.wait_ge(arrived[slot], slot_count(layer, g, GROUPS, s))
                else:
                    act.wait_ge(transposed, turned_tiles(layer, s, c) + 1)
                if layer == 0 and is_kept(g):
                    if kept_index(g) > 0 or not isinstance(s, int):
                        act.wait_ge(kept_out[i], kept_tiles(s, g) // BANKS * 16)
                    nc.scalar.activation(kept[:, i], psum[:, i], ACT.Copy).then_inc(kept_ready, 1)
                if layer == 2 and isinstance(s, int) and c < BANKS:
                    act.wait_ge(wide_products, WIDES * WIDE_TILES)
                elif n >= BANKS or not isinstance(s, int):
                    act.wait_ge(products, n + s * BLOCKS - BANKS + 1)
                tile = ring[:, (LOADS[layer] + g) % RING, c % PER_CHUNK] if loaded(layer, c) else psum[:, i]
                sums = {"accum_out": col_parts[:, c, bass.ds(s, 1)]} if layer == 0 else {}
                nc.scalar.activation(parts[:, i, 0], tile, ACT.Copy, **sums).then_inc(high_ready, 1)

            def copy_acc(layer, t):
                act.wait_ge(products, TURN[layer] + (t + 1) * BLOCKS)
                if layer != 0 or not isinstance(t, int):
                    act.wait_ge(y_ready, unit(layer, t))
                nc.scalar.activation(acc_sb[:, 0:SUPER], psum[:, ACC], ACT.Copy).then_inc(acc_copied, 1)

            def root(layer, t):
                act.wait_ge(var_ready, unit(layer, t) + 1)
                nc.scalar.activation(sd[:], var[:], ACT.Sqrt).then_inc(sd_ready, 1)

            def split(layer, t):
                if layer == 1:
                    act.wait_ge(scaled_ready, t + 1)
                else:
                    act.wait_ge(new_ready, unit(layer, t) + 1)
                nc.scalar.activation(x_high[(layer + 1) % 2][:, bass.ds(t * BLOCK_ROWS, BLOCK_ROWS), :],
                                     (u if layer == 1 else x_new[:]), ACT.Copy).then_inc(split_high, 1)

            def close(block, pending, wide):
                for layer, t, _, _, stage in stages(block - 1, pending, wide):
                    if stage == VARIANCE:
                        root(layer, t)
                    if stage == TIMES_D and layer != 3:
                        split(layer, t)

            def superblock(layer, s, pending):
                for c in range(BLOCKS):
                    high_part(layer, s, c)
                    if c == LAG and pending and pending[0] == layer:
                        copy_acc(layer, pending[1])
                    close(c, pending, False)

            def wide_high_parts(q, b):
                n = LOADS[1] + b // 2
                if b % 2 == 0:
                    act.wait_ge(arrived[n % RING], slot_count(1, b // 2, BLOCKS // 2, q))
                for h in range(HALVES):
                    tile = b * HALVES + h
                    if tile < BANKS and isinstance(q, int):
                        act.wait_ge(products, SUPERS * BLOCKS)
                    else:
                        act.wait_ge(wide_products, q * WIDE_TILES + tile - BANKS + 1)
                    nc.scalar.activation(parts[:, tile % BANKS, 0], wide_tile(n, b, h), ACT.Copy)\
                        .then_inc(wide_high, 1)

            def copy_wide(q):
                act.wait_ge(wide_products, (q + 1) * WIDE_TILES)
                act.wait_ge(y_ready, unit(1, 2 * q))
                for h in range(HALVES):
                    last = nc.scalar.activation(acc_sb[:, h * 512:(h + 1) * 512], psum[:, h], ACT.Copy)
                last.then_inc(wide_copied, 1)

            act.wait_ge(const_in, 16 * 8)
            for q in range(RING):
                act.wait_ge(arrived[q], 16)
                to = x_high[0][:, q * (BLOCKS // RING):(q + 1) * (BLOCKS // RING)].rearrange("p b f -> p (b f)")
                nc.scalar.activation(to, ring[:, q].rearrange("p r c -> p (r c)"), ACT.Identity, scale=a_bc[:])\
                    .then_inc(x0_high_ready, 1)

            superblock(0, 0, None)
            with act.Fori(1, SUPERS) as s:
                superblock(0, s, (0, s - 1, None))
            copy_acc(0, SUPERS - 1)
            for b in range(BLOCKS):
                wide_high_parts(0, b)
                close(b, (0, SUPERS - 1, None), True)
                if b == FACTORS_AT + 2:
                    act.wait_ge(factors, 7)
                    nc.scalar.activation(small[:, 1], small[:, 0], ACT.Sqrt).then_inc(factor_root, 1)
            with act.Fori(1, WIDES) as q:
                for b in range(BLOCKS):
                    wide_high_parts(q, b)
                    if b == 0:
                        copy_wide(q - 1)
                    close(b, (1, 2 * q - 2, None), True)
            copy_wide(WIDES - 1)
            superblock(2, 0, (1, SUPERS - 2, None))
            with act.Fori(1, SUPERS) as s:
                superblock(2, s, (2, s - 1, None))
            copy_acc(2, SUPERS - 1)
            superblock(3, 0, (2, SUPERS - 1, None))
            with act.Fori(1, SUPERS) as s:
                superblock(3, s, (3, s - 1, None))
            copy_acc(3, SUPERS - 1)
            root(3, SUPERS - 1)

        @block.vector
        def _(dve):
            def low_part(layer, s, c):
                i, g = c % BANKS, c // PER_CHUNK
                dve.wait_ge(high_ready, TURN[layer] + s * BLOCKS + c + 1)
                tile = ring[:, (LOADS[layer] + g) % RING, c % PER_CHUNK] if loaded(layer, c) else psum[:, i]
                nc.vector.tensor_tensor(parts[:, i, 1], tile, parts[:, i, 0].bitcast(F32), ALU.subtract)\
                    .then_inc(low_ready, 1)

            def row_sums(s, g):
                n = LOADS[0] + g
                dve.wait_ge(arrived[n % RING], slot_count(0, g, GROUPS, s))
                dve.wait_ge(rows_pool, s * (GROUPS - 1) + max(g, 1))
                nc.vector.tensor_reduce(row_parts[:, :, g, bass.ds(s, 1)].rearrange("p r a -> p (r a)"),
                                        ring[:, n % RING, 0:2], AX.X, ALU.add)\
                    .then_inc(rows_dve, 1)

            def rows(tensor, t):
                return tensor[:, bass.ds(t * BLOCK_ROWS, BLOCK_ROWS)]

            def unit_row_sums(t):
                dve.wait_ge(rows_dve, (t + 1) * GROUPS)
                nc.vector.tensor_reduce(row_sum[:, bass.ds(t * BLOCK_ROWS, 2)],
                                        row_parts[:, :, :, bass.ds(t, 1)].rearrange("p r g a -> p r (g a)"),
                                        AX.X, ALU.add)
                dve.wait_ge(rows_pool, (t + 1) * (GROUPS - 1))
                nc.vector.tensor_reduce(row_sum[:, bass.ds(t * BLOCK_ROWS + 2, 2)], row_acc[:], AX.X, ALU.add)\
                    .then_inc(rows_done, 1)

            def degree(t, second):
                def after(k):
                    dve.wait_ge(deg_steps, t * DEG_STEPS + k)

                if not second:
                    dve.wait_ge(rows_done, t + 1)
                    nc.vector.tensor_scalar(deg[:, 0], rows(row_sum, t), a_bc[:], one_minus_a[:], ALU.mult, ALU.add)\
                        .then_inc(deg_steps, 1)
                    after(1)
                    nc.vector.tensor_scalar(deg[:, 1], deg[:, 0], 0.0, None, ALU.is_equal).then_inc(deg_steps, 1)
                    after(2)
                    nc.vector.tensor_tensor(deg[:, 2], deg[:, 0], deg[:, 1], ALU.add).then_inc(deg_steps, 1)
                    return
                after(3)
                nc.vector.reciprocal(deg[:, 0], deg[:, 2]).then_inc(deg_steps, 1)
                nc.vector.tensor_scalar(deg[:, 4], deg[:, 1], -1.0, 1.0, ALU.mult, ALU.add).then_inc(deg_steps, 1)
                after(5)
                nc.vector.tensor_tensor(deg[:, 3], deg[:, 0], deg[:, 4], ALU.mult).then_inc(deg_steps, 1)

            def scale(layer, t, parity, pair):
                dve.wait_ge(y_ready, unit(layer, t) + 1)
                if layer == 0:
                    dve.wait_ge(deg_steps, (t + 1) * DEG_STEPS)
                    by = deg[:, 3]
                elif layer == 2:
                    by = rows(d_half, t)
                    if isinstance(t, int) and t == 0:
                        dve.wait_ge(split_done, unit(2, 0))
                else:
                    by = rows(col_factor if layer == 1 else degree3, t)
                if layer == 1:
                    dve.wait_ge(res_in[parity], res_value(1, pair, parity))
                    dve.wait_ge(split_done, unit(1, t))
                for r in range(BLOCK_ROWS):
                    plus = x_res[parity][:, r] if layer == 1 else bias[:, {0: 0, 2: 1, 3: 2}[layer]]
                    last = nc.vector.scalar_tensor_tensor(u[:, r, :], psum[:, Y + parity, r * P:(r + 1) * P],
                                                          by[:, r:r + 1], plus, ALU.mult, ALU.add)
                last.then_inc(y_used, 1)

            def residual(layer, t):
                dve.wait_ge(y_used, unit(layer, t) + 1)
                dve.wait_ge(res_in[0], res_value(layer, t, 0))
                if layer == 0:
                    done = nc.vector.scalar_tensor_tensor(u, u, 0.0, x_res[0][:], ALU.max, ALU.add)
                else:
                    done = nc.vector.tensor_tensor(u, u, x_res[0][:], ALU.add)
                done.then_inc(res_used, 1)

            def close(block, pending, wide):
                for layer, t, parity, pair, stage in stages(block, pending, wide):
                    close_stage(layer, t, parity, pair, stage)

            def close_stage(layer, t, parity, pair, stage):
                    n = unit(layer, t)
                    if stage == DEGREE and layer == 0:
                        degree(t, False)
                    if stage == DEGREE2 and layer == 0:
                        degree(t, True)
                    if stage == SCALE:
                        scale(layer, t, parity, pair)
                    if stage == RESIDUAL and layer != 1:
                        residual(layer, t)
                    if stage == STATS:
                        if layer == 1:
                            dve.wait_ge(y_used, n + 1)
                        else:
                            dve.wait_ge(res_used, turned(layer, t) + 1)
                        for r in range(BLOCK_ROWS):
                            last = nc.vector.bn_stats(stats[:, r], u[:, r, :])
                        last.then_inc(stats_ready, 1)
                    if stage == MOMENTS:
                        dve.wait_ge(stats_ready, n + 1)
                        nc.vector.tensor_copy(rt[:, 0], stats[:, :, 0])
                        for r in range(BLOCK_ROWS):
                            last = nc.vector.bn_aggr(moments[:, r], stats[:, r])
                        last.then_inc(moments_ready, 1)
                    if stage == VARIANCE:
                        dve.wait_ge(moments_ready, n + 1)
                        nc.vector.tensor_scalar(var[:], moments[:, :, 1], EPS, None, ALU.add).then_inc(var_ready, 1)
                    if stage == ROOT:
                        dve.wait_ge(sd_ready, n + 1)
                        nc.vector.reciprocal(rs[:], sd[:]).then_inc(root_steps, 1)
                        dve.wait_ge(root_steps, n * ROOT_STEPS + 1)
                        nc.vector.tensor_tensor(rt[:, 0], var[:], rs[:], ALU.mult).then_inc(root_steps, 1)
                        dve.wait_ge(root_steps, n * ROOT_STEPS + 2)
                        nc.vector.tensor_tensor(rt[:, 1], rt[:, 0], rs[:], ALU.mult).then_inc(root_steps, 1)
                    if stage == ROOT2:
                        dve.wait_ge(root_steps, n * ROOT_STEPS + 3)
                        nc.vector.tensor_scalar(rt[:, 2], rt[:, 1], -0.5, 1.5, ALU.mult, ALU.add)\
                            .then_inc(root_steps, 1)
                        dve.wait_ge(root_steps, n * ROOT_STEPS + 4)
                        nc.vector.tensor_tensor(rt[:, 3], rt[:, 2], rs[:], ALU.mult).then_inc(root_steps, 1)
                    if stage == NORM:
                        dve.wait_ge(root_steps, (n + 1) * ROOT_STEPS)
                        if not (layer == 0 and isinstance(t, int) and t == 0):
                            dve.wait_ge(stored, 16 * n)
                            dve.wait_ge(split_done, min_split(layer, t))
                        for r in range(BLOCK_ROWS):
                            last = nc.vector.tensor_scalar(x_new[:, r], u[:, r, :], moments[:, r, 0:1],
                                                           rt[:, 3, r:r + 1], ALU.subtract, ALU.mult)
                        last.then_inc(new_ready, 1)
                    if stage == TIMES_D and layer == 1:
                        dve.wait_ge(new_ready, n + 1)
                        by = rows(d_half, t)
                        for r in range(BLOCK_ROWS):
                            last = nc.vector.tensor_scalar(u[:, r, :], x_new[:, r], by[:, r:r + 1], None,
                                                           ALU.mult)
                        last.then_inc(scaled_ready, 1)
                    if stage == LOW and layer != 3:
                        dve.wait_ge(split_high, n + 1)
                        span = bass.ds(t * BLOCK_ROWS, BLOCK_ROWS)
                        nc.vector.tensor_tensor(x_low[(layer + 1) % 2][:, span, :],
                                                (u if layer == 1 else x_new[:]),
                                                x_high[(layer + 1) % 2][:, span, :].bitcast(F32), ALU.subtract)\
                            .then_inc(split_done, 1)

            def min_split(layer, t):
                return unit(3, 0) if layer == 3 else unit(layer, t)

            def diagonal(s):
                dve.wait_ge(products, TURN[3] + s * BLOCKS)
                for r in range(BLOCK_ROWS):
                    last = nc.vector.tensor_scalar(diag[:, r], identity[:],
                                                   rows(beta_col, s)[:, r:r + 1], None, ALU.mult)
                last.then_inc(diag_ready, 1)

            def superblock(layer, s, pending):
                for c in range(BLOCKS):
                    if c == 0 and layer == 0 and pending:
                        unit_row_sums(pending[1])
                    low_part(layer, s, c)
                    if layer == 0 and c % PER_CHUNK == PER_CHUNK - 1:
                        row_sums(s, c // PER_CHUNK)
                    if layer == 3 and c == 40:
                        diagonal(s)
                    close(c, pending, False)

            def wide_low_parts(q, b):
                for h in range(HALVES):
                    tile = b * HALVES + h
                    i = tile % BANKS
                    dve.wait_ge(wide_high, q * WIDE_TILES + tile + 1)
                    nc.vector.tensor_tensor(parts[:, i, 1], wide_tile(LOADS[1] + b // 2, b, h),
                                            parts[:, i, 0].bitcast(F32), ALU.subtract).then_inc(wide_low, 1)

            def layer_factors(part):
                def after(k):
                    dve.wait_ge(factors, k)

                if part == 0:
                    nc.vector.tensor_reduce(col_sum[:], col_parts[:], AX.X, ALU.add).then_inc(factors, 1)
                    after(1)
                    nc.vector.tensor_scalar(small[:, 2], col_sum[:], 0.0, None, ALU.is_equal).then_inc(factors, 1)
                    after(2)
                    nc.vector.tensor_tensor(small[:, 3], col_sum[:], small[:, 2], ALU.add).then_inc(factors, 1)
                    after(3)
                    nc.vector.reciprocal(small[:, 4], small[:, 3]).then_inc(factors, 1)
                    nc.vector.tensor_scalar(small[:, 5], small[:, 2], -1.0, 1.0, ALU.mult, ALU.add)\
                        .then_inc(factors, 1)
                    after(5)
                    nc.vector.tensor_tensor(col_factor[:], small[:, 4], small[:, 5], ALU.mult).then_inc(factors, 1)
                    nc.vector.tensor_scalar(small[:, 0], row_sum[:], 1e-8, None, ALU.add).then_inc(factors, 1)
                if part == 1:
                    nc.vector.tensor_tensor(small[:, 6], row_sum[:], beta_col[:], ALU.add).then_inc(factors, 1)
                    after(8)
                    nc.vector.reciprocal(degree3[:], small[:, 6]).then_inc(factors, 1)
                    dve.wait_ge(factor_root, 1)
                    nc.vector.reciprocal(small[:, 7], small[:, 1]).then_inc(factors, 1)
                    after(10)
                    nc.vector.tensor_tensor(small[:, 8], small[:, 0], small[:, 7], ALU.mult).then_inc(factors, 1)
                    after(11)
                    nc.vector.tensor_tensor(small[:, 9], small[:, 8], small[:, 7], ALU.mult).then_inc(factors, 1)
                    after(12)
                    nc.vector.tensor_scalar(small[:, 10], small[:, 9], -0.5, 1.5, ALU.mult, ALU.add)\
                        .then_inc(factors, 1)
                    after(13)
                    nc.vector.tensor_tensor(d_half[:], small[:, 10], small[:, 7], ALU.mult).then_inc(factors, 1)
                    after(14)

            dve.wait_ge(const_in, 16 * 8)
            nc.vector.tensor_scalar(one_minus_a[:], a_bc[:], -1.0, 1.0, ALU.mult, ALU.add).then_inc(setup_dve, 1)
            dve.wait_ge(setup_dve, 1)
            dve.wait_ge(made, 2)
            nc.vector.tensor_scalar(diag0[:], identity[:], one_minus_a[:], None, ALU.mult).then_inc(setup_dve, 1)
            dve.wait_ge(setup_pe, 1)
            for i in range(2):
                nc.vector.tensor_copy(w_mov[:, i], psum[:, Y, i * P:(i + 1) * P]).then_inc(setup_dve, 1)
            nc.vector.tensor_copy(beta_col[:], psum[:, Y, 2 * P:2 * P + BLOCKS]).then_inc(setup_dve, 1)
            dve.wait_ge(setup_dve, 5)
            for q in range(RING):
                span = slice(q * (BLOCKS // RING), (q + 1) * (BLOCKS // RING))
                dve.wait_ge(x0_high_ready, q + 1)
                nc.vector.scalar_tensor_tensor(x_low[0][:, span].rearrange("p b f -> p (b f)"),
                                               ring[:, q].rearrange("p r c -> p (r c)"), a_bc[:],
                                               x_high[0][:, span].rearrange("p b f -> p (b f)").bitcast(F32),
                                               ALU.mult, ALU.subtract).then_inc(x0_ready, 1)

            superblock(0, 0, None)
            with dve.Fori(1, SUPERS) as s:
                superblock(0, s, (0, s - 1, None))
            for b in range(BLOCKS):
                wide_low_parts(0, b)
                if b == 0:
                    unit_row_sums(SUPERS - 1)
                close(b, (0, SUPERS - 1, None), True)
                if b == FACTORS_AT:
                    layer_factors(0)
                if b == FACTORS_AT + 4:
                    layer_factors(1)
            with dve.Fori(1, WIDES) as q:
                for b in range(BLOCKS):
                    wide_low_parts(q, b)
                    close(b, (1, 2 * q - 2, q - 1), True)
            superblock(2, 0, (1, SUPERS - 2, WIDES - 1))
            with dve.Fori(1, SUPERS) as s:
                superblock(2, s, (2, s - 1, None))
            superblock(3, 0, (2, SUPERS - 1, None))
            with dve.Fori(1, SUPERS) as s:
                superblock(3, s, (3, s - 1, None))
            for stage in range(LOW + 1):
                close_stage(3, SUPERS - 1, 0, None, stage)

        @block.gpsimd
        def _(pool):
            nc.gpsimd.memset(identity[:], 0.0).then_inc(made, 1)
            pool.wait_ge(made, 1)
            nc.gpsimd.affine_select(out=identity[:], in_=identity[:], compare_op=ALU.not_equal, fill=1.0, base=0,
                                    pattern=[[-1, P]], channel_multiplier=1).then_inc(made, 1)

            def row_sums(s):
                for g in range(GROUPS):
                    n = LOADS[0] + g
                    pool.wait_ge(arrived[n % RING], slot_count(0, g, GROUPS, s))
                    if g == 0:
                        continue
                    if g == 1:
                        before = ring[:, LOADS[0] % RING, 2:4]
                        if not isinstance(s, int):
                            pool.wait_ge(rows_done, s)
                    else:
                        before = row_acc[:]
                        pool.wait_ge(rows_pool, s * (GROUPS - 1) + g - 1)
                    nc.gpsimd.tensor_tensor(row_acc[:], before, ring[:, n % RING, 2:4], ALU.add)\
                        .then_inc(rows_pool, 1)

            row_sums(0)
            with pool.Fori(1, SUPERS) as s:
                row_sums(s)


_ARGS = ["x", "adj", "L0_gnn_alpha", "L0_gnn_W", "L0_gnn_b", "L2_gnn_W", "L2_gnn_b", "L3_gnn_kernel",
         "L3_gnn_bias", "L3_gnn_beta"]


def kernel(x, adj, L0_gnn_t, L0_gnn_alpha, L0_gnn_W, L0_gnn_b, L2_gnn_W, L2_gnn_b, L3_gnn_kernel,
           L3_gnn_bias, L3_gnn_beta):
    import numpy as np
    import concourse.bacc as bacc
    from concourse.bass_utils import run_bass_kernel_spmd

    given = [x, adj, L0_gnn_alpha, L0_gnn_W, L0_gnn_b, L2_gnn_W, L2_gnn_b, L3_gnn_kernel, L3_gnn_bias,
             L3_gnn_beta]
    nc = bacc.Bacc("TRN2", target_bir_lowering=False, num_devices=1)
    arrays, args = {}, []
    for name, value in zip(_ARGS, given):
        a = np.ascontiguousarray(value)
        arrays[f"in_{name}"] = a
        args.append(nc.dram_tensor(f"in_{name}", a.shape, mybir.dt.from_np(a.dtype), kind="ExternalInput").ap())
    out = nc.dram_tensor("out", x.shape, mybir.dt.float32, kind="ExternalOutput").ap()
    plain = [nc.dram_tensor(f"x{i + 1}_plain", x.shape, mybir.dt.float32, kind="Internal").ap() for i in range(3)]
    rows, per_load = 512, 4
    turned = nc.dram_tensor("a_turned", (x.shape[0] // rows, KEPT_GROUPS, P, per_load, rows),
                            mybir.dt.float32, kind="Internal").ap()
    build(nc, *args, out, plain, turned)
    return run_bass_kernel_spmd(nc, [arrays], core_ids=[0]).results[0]["out"]
```

```python
import concourse.bass as bass
from concourse import mybir
from contextlib import ExitStack

P = 128
EPS = 1e-5
KEPT_GROUPS = 8


def build(nc: bass.Bass, x_in, adj, alpha, W0, b0, W2, b2, K3, b3, beta, out, x2_plain, a_turned, early):
    F32, F32R = mybir.dt.float32, mybir.dt.float32r
    ALU, ACT, AX = mybir.AluOpType, mybir.ActivationFunctionType, mybir.AxisListType

    N, F = x_in.shape
    BLOCKS = N // P
    BLOCK_ROWS = 4
    SUPER = BLOCK_ROWS * P
    SUPERS = N // SUPER
    CHUNK = 512
    GROUPS = N // CHUNK
    PER_CHUNK = CHUNK // P
    WIDE = 1024
    WIDES = N // WIDE
    RING = 4
    BANKS = 4
    LAG = 3
    HALVES = WIDE // 512
    WIDE_TILES = BLOCKS * HALVES
    KEPT = KEPT_GROUPS
    DIAGONAL_AT = -4
    SUM_AT = (LAG, LAG + 1)
    FACTORS_AT = 44

    def half_at(n):
        return n // 2 + min(8, n // 4)

    def is_kept(g):
        return (g + 1) * KEPT // GROUPS > g * KEPT // GROUPS

    QUARTERS = 4
    QUARTER = SUPERS // QUARTERS
    assert QUARTER % RING == 0 and SUPERS == GROUPS

    def order(layer, quarter):
        before = quarter * QUARTER
        if layer == 2:
            others = range(before, GROUPS - 1)
            at = {g: (g - before + 0.5) / len(others) for g in others} | {g: (g + 1) / before for g in range(before)}
            groups = sorted(at, key=at.get)
            late = [g for g in groups if not keeps(2, quarter, g)][-(RING - 2):]
            return [g for g in groups if g not in late] + late + [GROUPS - 1]
        return list(range(before if layer == 3 else 0, GROUPS))

    def keeps(layer, quarter, g):
        if layer == 0:
            return is_kept(g)
        return layer == 2 and not is_kept(g) and g >= quarter * QUARTER and (quarter > 0 or g % 4 == 2)

    def loads_before(layer, quarter, s):
        if layer != 3:
            return s * GROUPS
        start = quarter * QUARTER
        return (sum(QUARTER * len(order(3, k)) for k in range(quarter))
                + (s - start) * len(order(3, quarter)))

    LOADS = {0: RING, 1: RING + SUPERS * GROUPS}
    LOADS[2] = LOADS[1] + WIDES * BLOCKS // 2
    LOADS[3] = LOADS[2] + SUPERS * GROUPS
    TURN = {0: 0, 2: SUPERS * BLOCKS, 3: 2 * SUPERS * BLOCKS}

    ctx = ExitStack()
    with ctx:
        def sb(name, shape, dt=F32):
            return ctx.enter_context(nc.sbuf_tensor(name, shape, dt))

        def sem(name):
            return ctx.enter_context(nc.semaphore(name))

        x_high = [sb(f"x_high{i}", [P, BLOCKS, F], F32R) for i in range(2)]
        x_low = [sb(f"x_low{i}", [P, BLOCKS, F], F32R) for i in range(2)]
        ring = sb("ring", [P, RING, BLOCK_ROWS, CHUNK])
        parts = sb("parts", [P, BANKS, 2, 512], F32R)
        acc_sb = sb("acc_sb", [P, WIDE])
        w_nat = acc_sb[:, 0:2 * F].rearrange("p (w f) -> p w f", w=2)
        beta_rows = acc_sb[0:BLOCKS, 2 * F:2 * F + P]
        diag0 = acc_sb[:, 512:512 + P]
        x_res = [sb(f"x_res{i}", [P, BLOCK_ROWS, F]) for i in range(2)]
        kept = sb("kept", [P, BANKS, 512])
        x_new = sb("x_new", [P, BLOCK_ROWS, F])
        identity = sb("identity", [P, P])
        w_mov = sb("w_mov", [P, 3, F])
        bias = sb("bias", [P, 3, F])
        a_bc = sb("a_bc", [P, 1])
        one_minus_a = sb("one_minus_a", [P, 1])
        beta_col = sb("beta_col", [P, BLOCKS])
        row_parts = sb("row_parts", [P, GROUPS, SUPERS])
        row_acc = sb("row_acc", [P, BLOCK_ROWS - 1, CHUNK // 2])
        row_sum = sb("row_sum", [P, BLOCKS])
        col_parts = sb("col_parts", [P, BLOCKS, SUPERS])
        diag = col_parts[:].rearrange("p b s -> p (b s)")[:, 0:SUPER].rearrange("p (b q) -> p b q", q=P)
        col_sum = sb("col_sum", [P, BLOCKS])
        col_factor = sb("col_factor", [P, BLOCKS])
        degree3 = sb("degree3", [P, BLOCKS])
        d_half = sb("d_half", [P, BLOCKS])
        small = row_acc[:].rearrange("p a (k b) -> p (a k) b", b=BLOCKS)
        deg = sb("deg", [P, 5, BLOCK_ROWS])
        stats = sb("stats", [P, BLOCK_ROWS, 6])
        moments = sb("moments", [P, BLOCK_ROWS, 2])
        var = sb("var", [P, BLOCK_ROWS])
        sd = sb("sd", [P, BLOCK_ROWS])
        rs = sb("rs", [P, BLOCK_ROWS])
        rt = sb("rt", [P, 4, BLOCK_ROWS])

        psum = ctx.enter_context(nc.psum_tensor("psum", [P, 8, 512], F32))
        ACC, Y, ACC2, EARLY = 4, 5, 6, 7
        u01 = psum[:, EARLY].rearrange("p (b f) -> p b f", f=F)
        u23 = x_res[1][:]
        early_sums = row_acc[:, 0:2].rearrange("p a k -> p (a k)")
        EARLY_IN = 2

        arrived = [sem(f"arrived{i}") for i in range(RING)]
        const_in = sem("const_in")
        made = sem("made")
        setup_pe = sem("setup_pe")
        setup_dve = sem("setup_dve")
        x0_high_ready = sem("x0_high_ready")
        x0_ready = sem("x0_ready")
        transposed = sem("transposed")
        high_ready = sem("high_ready")
        low_ready = sem("low_ready")
        products = sem("products")
        half_copied = sem("half_copied")
        acc_copied = sem("acc_copied")
        y_ready = sem("y_ready")
        y_used = sem("y_used")
        res_in = sem("res_in")
        res_made = sem("res_made")
        res_used = sem("res_used")
        diag_ready = sem("diag_ready")
        wide_high = sem("wide_high")
        wide_low = sem("wide_low")
        wide_products = sem("wide_products")
        wide_copied = sem("wide_copied")
        early_copied = sem("early_copied")
        early_out = sem("early_out")
        early_in = sem("early_in")
        kept_ready = sem("kept_ready")
        kept_out = [sem(f"kept_out{i}") for i in range(BANKS)]
        rows_dve = sem("rows_dve")
        rows_pool = sem("rows_pool")
        rows_done = sem("rows_done")
        deg_steps = sem("deg_steps")
        stats_ready = sem("stats_ready")
        moments_ready = sem("moments_ready")
        var_ready = sem("var_ready")
        sd_ready = sem("sd_ready")
        root_steps = sem("root_steps")
        new_ready = sem("new_ready")
        scaled_ready = sem("scaled_ready")
        split_high = sem("split_high")
        split_done = sem("split_done")
        stored = sem("stored")
        factors = sem("factors")
        factor_root = sem("factor_root")

        DEG_STEPS, ROOT_STEPS = 6, 5

        def column_block(layer, quarter, c):
            return order(layer, quarter)[c // PER_CHUNK] * PER_CHUNK + c % PER_CHUNK

        def loaded(layer, quarter, c):
            g = order(layer, quarter)[c // PER_CHUNK]
            return layer != 0 and is_kept(g) or layer == 3 and keeps(2, quarter, g)

        def tiles(layer, quarter, s):
            return TURN[layer] + loads_before(layer, quarter, s) * PER_CHUNK

        def turned_tiles(layer, quarter, s, c):
            def loads(k, until=None):
                return sum(not loaded(layer, k, j * PER_CHUNK) for j in range(len(order(layer, k)))[:until])

            start = quarter * QUARTER
            whole = {0: 0, 2: SUPERS * GROUPS, 3: SUPERS * (2 * GROUPS - KEPT)}[layer]
            whole += sum(QUARTER * loads(k) for k in range(quarter))
            return (whole + (s - start) * loads(quarter) + loads(quarter, c // PER_CHUNK)) * PER_CHUNK + c % PER_CHUNK

        def kept_tiles(layer, quarter, s, at):
            if layer == 0:
                return (s * KEPT + sum(is_kept(g) for g in range(at))) * PER_CHUNK

            def loads(k, until=None):
                return sum(keeps(2, k, g) for g in order(2, k)[:until])

            start = quarter * QUARTER
            before = SUPERS * KEPT + sum(QUARTER * loads(k) for k in range(quarter))
            return (before + (s - start) * loads(quarter) + loads(quarter, at)) * PER_CHUNK

        def kept_in_all():
            return kept_tiles(2, QUARTERS - 1, SUPERS, 0)

        def unit(layer, t):
            return layer * SUPERS + t

        def turned(layer, s):
            return TURN[layer] // BLOCKS + s

        def first(s):
            return isinstance(s, int) and s == 0

        def slot_count(layer, quarter, g, s):
            at = LOADS[layer] + g
            if layer != 3:
                return (s * (GROUPS // RING) + at // RING + 1) * 16
            start = quarter * QUARTER
            return ((s - start) * (len(order(3, quarter)) // RING)
                    + (at + loads_before(3, quarter, start)) // RING + 1) * 16

        def wait_for_x(engine, layer, t):
            before = SUPERS * (layer // 2)
            engine.wait_ge(res_made if layer % 2 else res_in, (before + t + 1) * (1 if layer % 2 else 16))

        DEGREE, DEGREE2, SCALE, RESIDUAL, STATS, MOMENTS, VARIANCE, ROOT, ROOT2, NORM, TIMES_D, LOW = range(12)
        STEPS = [(DEGREE, 0), (DEGREE2, 0), *((SCALE, r) for r in range(4)), (RESIDUAL, 0), (STATS, 0), (STATS, 1),
                 (MOMENTS, 0), (VARIANCE, 0), (ROOT, 0), (ROOT2, 0), *((NORM, r) for r in range(4)),
                 (TIMES_D, 0), (LOW, 0)]

        def alone(layer, quarter):
            steps = [x for x in STEPS if layer != 3 or x[0] not in (DEGREE, DEGREE2, TIMES_D, LOW)]
            n = len(order(layer, quarter)) * PER_CHUNK
            if layer == 2 and quarter > 0:
                places = range(8, n, 2)
            elif layer != 3:
                places = [c for c in range(8, n) if not is_kept(order(layer, quarter)[c // PER_CHUNK])]
            elif n > BLOCKS // 2:
                places = range(8, n, 2)
            else:
                places = sorted([*range(8, n)] * (1 if n > 16 else 2))
            return list(zip(places, steps, strict=False))

        PAIR_WIDE = [range(first, first + len(STEPS)) for first in (4, 34)]
        PAIR_ROWS = [range(first, first + len(STEPS)) for first in (4, 23)]

        def stages(block, pending, wide, quarter=0):
            if pending is None:
                return
            layer, t, pair = pending
            if layer != 1:
                for place, step in alone(layer, quarter):
                    if place == block:
                        yield layer, t, 0, t, step
                return
            for parity in range(2):
                places = (PAIR_WIDE if wide else PAIR_ROWS)[parity]
                if block in places:
                    yield layer, t + parity, parity, pair, STEPS[places.index(block)]

        def x0_quarter(q):
            return ring[:, q].rearrange("p r c -> p (r c)").rearrange("p (b f) -> p b f", f=F)

        adj_chunks = adj.rearrange("(s r p) c -> s p r c", r=BLOCK_ROWS, p=P)
        adj_wides = adj.rearrange("(k r p) (q c) -> k q p r c", r=2, p=P, c=WIDE)
        x_in_quarters = x_in.rearrange("(q b p) f -> q p b f", q=RING, p=P)
        x_units = {i: x.rearrange("(t b p) f -> t p b f", b=BLOCK_ROWS, p=P)
                   for i, x in ((0, x_in), (2, x2_plain), (4, out))}

        block = ctx.enter_context(nc.Block())

        @block.sync
        def _(sp):
            def store(layer, t):
                sp.wait_ge(new_ready, unit(layer, t) + 1)
                sp.dma_start(x_units[layer + 1][t], x_new[:]).then_inc(stored, 16)

            def keep(layer, quarter, s, at, counted=None):
                begin, i = counted or (0, s)
                for k in range(PER_CHUNK):
                    sp.wait_ge(kept_ready, kept_tiles(layer, quarter, s, at) + k + 1)
                    sp.dma_start(a_turned[begin:][i, order(layer, quarter)[at], :, k, :], kept[:, k])\
                        .then_inc(kept_out[k], 16)

            def next_x(layer, s):
                if layer == 2 and first(s):
                    sp.wait_ge(stored, 16 * SUPERS)
                    sp.wait_ge(y_used, unit(2, 0))
                if layer != 0 or not first(s):
                    sp.wait_ge(res_used, turned(layer, s))
                sp.dma_start(x_res[0][:], x_units[layer][s]).then_inc(res_in, 16)

            def superblock(layer, quarter, s, pending, counted=None):
                begin, k = counted or (0, s)
                chunks_from, turned_from = adj_chunks[begin:], a_turned[begin:]
                groups = order(layer, quarter)
                short = len(groups) == RING
                first_kept = groups.index(min(filter(is_kept, groups)))
                for j, g in enumerate(groups):
                    slot = (LOADS[layer] + j) % RING
                    if first(s) and j < RING and layer == 0:
                        sp.wait_ge(x0_ready, j + 1)
                    elif first(s) and j < RING and layer == 2:
                        sp.wait_ge(wide_low, WIDES * WIDE_TILES - 2 * HALVES * (RING - j - 1))
                    else:
                        until = j - RING + 1
                        if layer == 0:
                            sp.wait_ge(rows_dve, s * GROUPS + until)
                        else:
                            sp.wait_ge(low_ready, tiles(layer, quarter, s) + until * PER_CHUNK)
                    if first(s) and (layer == 3 and j == 0 or layer == 2 and j == first_kept):
                        for i in range(BANKS):
                            sp.wait_ge(kept_out[i], 16 * (SUPERS * KEPT if layer == 2 else kept_in_all() // BANKS))
                    of = (turned_from[k, g] if loaded(layer, quarter, j * PER_CHUNK)
                          else chunks_from[k, :, :, g * CHUNK:(g + 1) * CHUNK])
                    sp.dma_start(ring[:, slot], of).then_inc(arrived[slot], 16)
                    behind = j - RING + 1
                    if behind >= 0 and keeps(layer, quarter, groups[behind]):
                        keep(layer, quarter, s, behind, counted)
                    if behind < 0 and layer == 0 and not first(s) and is_kept(groups[behind]):
                        keep(0, 0, s - 1, behind + GROUPS)
                    if j == 8 and pending and pending[0] == 1:
                        store(1, SUPERS - 2)
                    if short:
                        if pending and j == RING - 1:
                            store(layer, s - 2)
                    elif j == min(len(groups) - 1, 13):
                        if pending and pending[0] in (1, 3):
                            layer_before, t, _ = pending
                            store(layer_before, SUPERS - 1 if layer_before == 1 else t)
                        if layer != 3:
                            next_x(layer, s)

            def wide_load(q, k):
                n = LOADS[1] + k
                if isinstance(q, int) and k < RING:
                    last = SUPERS * GROUPS - RING + k + 1
                    sp.wait_ge(rows_dve, last)
                else:
                    sp.wait_ge(wide_low, q * WIDE_TILES + 2 * HALVES * (k - RING + 1))
                sp.dma_start(ring[:, n % RING].rearrange("p r c -> p (r c)").rearrange("p (r c) -> p r c", r=2),
                             adj_wides[k, q]).then_inc(arrived[n % RING], 16)

            for to, of in ((a_bc[:], alpha.partition_broadcast(P)), (bias[:, 0], b0.partition_broadcast(P)),
                           (bias[:, 1], b2.partition_broadcast(P)), (bias[:, 2], b3.partition_broadcast(P)),
                           (w_nat[:, 0], W0), (w_nat[:, 1], W2), (w_mov[:, 2], K3),
                           (beta_rows, beta.rearrange("(b p) -> b p", p=P))):
                sp.dma_start(to, of).then_inc(const_in, 16)
            for q in range(RING):
                sp.dma_start(x0_quarter(q), x_in_quarters[q]).then_inc(arrived[q], 16)

            superblock(0, 0, 0, None)
            with sp.Fori(1, SUPERS) as s:
                superblock(0, 0, s, (0, s - 1, None))
            for k in range(BLOCKS // 2):
                wide_load(0, k)
                if k < RING - 1 and is_kept(GROUPS + k - RING + 1):
                    keep(0, 0, SUPERS - 1, GROUPS + k - RING + 1)
            with sp.Fori(1, WIDES) as q:
                for k in range(BLOCKS // 2):
                    wide_load(q, k)
                    if k == 20:
                        store(1, 2 * q - 2)
                store(1, 2 * q - 1)
            for layer, pending in ((2, (1, SUPERS - 2, None)), (3, (2, SUPERS - 1, None))):
                superblock(layer, 0, 0, pending)
                for quarter in range(QUARTERS):
                    start, stop = quarter * QUARTER, (quarter + 1) * QUARTER
                    if len(order(layer, quarter)) == RING:
                        for s in range(start, stop):
                            superblock(layer, quarter, s, (layer, s - 1, None) if s > start else None)
                        continue
                    begin = max(start, 1)
                    with sp.Fori(0, stop - begin) as k:
                        superblock(layer, quarter, k + begin, (layer, k + begin - 1, None), (begin, k))
            store(3, SUPERS - 2)
            store(3, SUPERS - 1)
            sp.wait_ge(stored, 16 * 2 * SUPERS)

        @block.tensor
        def _(pe):
            def turn(layer, quarter, s, c):
                g = c // PER_CHUNK
                slot = (LOADS[layer] + g) % RING
                if c % PER_CHUNK == 0:
                    pe.wait_ge(arrived[slot], slot_count(layer, quarter, g, s))
                if layer == 2 and first(s) and c == 0:
                    pe.wait_ge(wide_copied, WIDES)
                if layer != 0 or c >= BANKS or not first(s):
                    pe.wait_ge(low_ready, tiles(layer, quarter, s) + c - BANKS + 1)
                at = (c % PER_CHUNK) * P
                for r in range(BLOCK_ROWS):
                    last = nc.tensor.transpose(psum[:, c % BANKS, r * P:(r + 1) * P],
                                               ring[:, slot, r, at:at + P], identity[:])
                last.then_inc(transposed, 1)

            def products_of(acc, x, at, i, start, stop):
                high, low = x_high[x][:, at], x_low[x][:, at]
                nc.tensor.matmul(acc, high, parts[:, i, 0], start=start, stop=False, skip_group_check=True)
                nc.tensor.matmul(acc, high, parts[:, i, 1], start=False, stop=False, skip_group_check=True)
                return nc.tensor.matmul(acc, low, parts[:, i, 0], start=False, stop=stop, skip_group_check=True)

            def multiply(layer, quarter, s, c):
                half = len(order(layer, quarter)) * PER_CHUNK // 2
                i = c % BANKS
                if c == 0 and not (layer == 0 and first(s)):
                    pe.wait_ge(half_copied, turned(layer, s))
                if c == half and not (layer == 0 and first(s)):
                    pe.wait_ge(acc_copied, 2 * turned(layer, s))
                    if layer == 2 and first(s):
                        pe.wait_ge(y_used, unit(2, 0))
                if first(s) and c >= 0:
                    if layer == 0 and c % (BLOCKS // RING) == 0:
                        pe.wait_ge(x0_ready, c // (BLOCKS // RING) + 1)
                    if layer != 0 and c % BLOCK_ROWS == 0:
                        pe.wait_ge(split_done, unit(layer - 1, column_block(layer, 0, c) // BLOCK_ROWS) + 1)
                pe.wait_ge(low_ready, tiles(layer, quarter, s) + c + 1)
                if c < 0:
                    products_of(psum[:, ACC2], layer % 2, BLOCKS + c, i, False, c == -1).then_inc(products, 1)
                    return
                at = column_block(layer, quarter, c)
                acc = psum[:, ACC if c < half else ACC2]
                if c == 2 * half + DIAGONAL_AT and layer != 2:
                    wait_for_x(pe, layer, s)
                    if layer == 3:
                        pe.wait_ge(diag_ready, s + 1)
                    for r in range(BLOCK_ROWS):
                        nc.tensor.matmul(acc[:, r * P:(r + 1) * P], x_res[0][:, r],
                                         diag0[:] if layer == 0 else diag[:, r], start=False, stop=False,
                                         skip_group_check=True)
                early_blocks = quarter * QUARTER * PER_CHUNK
                if layer == 2 and at < early_blocks:
                    if at % PER_CHUNK == 0:
                        pe.wait_ge(split_done, unit(2, at // PER_CHUNK) + 1)
                    products_of(psum[:, EARLY], 1, at, i, at == 0, at == early_blocks - 1)
                products_of(acc, layer % 2, at, i, c in (0, half), c == half - 1).then_inc(products, 1)

            def project(layer, t):
                pe.wait_ge(acc_copied, 2 * (turned(layer, t) + 1))
                if layer != 0 or not isinstance(t, int) or t > 0:
                    pe.wait_ge(y_used, unit(layer, t))
                for r in range(BLOCK_ROWS):
                    last = nc.tensor.matmul(psum[:, Y, r * P:(r + 1) * P], acc_sb[:, r * P:(r + 1) * P],
                                            w_mov[:, {0: 0, 2: 1, 3: 2}[layer]], start=True, stop=True)
                last.then_inc(y_ready, 1)

            def turn_back(q):
                pe.wait_ge(wide_copied, q + 1)
                for parity in range(2):
                    pe.wait_ge(y_used, unit(1, 2 * q - 1 + parity))
                    for r in range(BLOCK_ROWS):
                        at = parity * SUPER + r * P
                        last = nc.tensor.transpose(psum[:, Y + parity, r * P:(r + 1) * P],
                                                   acc_sb[:, at:at + P], identity[:])
                    last.then_inc(y_ready, 1)

            def superblock(layer, quarter, s, pending):
                for c in range(len(order(layer, quarter)) * PER_CHUNK):
                    if not loaded(layer, quarter, c):
                        turn(layer, quarter, s, c)
                    if c >= LAG or not first(s):
                        multiply(layer, quarter, s, c - LAG)
                    if c == 7 and pending:
                        if pending[0] == 1:
                            turn_back(WIDES - 1)
                        else:
                            project(*pending)

            def last_products(layer):
                for c in range(-LAG, 0):
                    multiply(layer, QUARTERS - 1, SUPERS, c)

            def wide_block(q, b):
                if b == 0 and isinstance(q, int):
                    pe.wait_ge(low_ready, SUPERS * BLOCKS)
                elif b == 0:
                    pe.wait_ge(wide_copied, q)
                if b % BLOCK_ROWS == 0 and isinstance(q, int):
                    pe.wait_ge(split_done, b // BLOCK_ROWS + 1)
                for h in range(HALVES):
                    i = (b * HALVES + h) % BANKS
                    pe.wait_ge(wide_low, q * WIDE_TILES + b * HALVES + h + 1)
                    nc.tensor.matmul(psum[:, h], x_high[1][:, b], parts[:, i, 0], start=(b == 0), stop=False)
                    nc.tensor.matmul(psum[:, h], x_high[1][:, b], parts[:, i, 1], start=False, stop=False)
                    nc.tensor.matmul(psum[:, h], x_low[1][:, b], parts[:, i, 0], start=False,
                                     stop=(b == BLOCKS - 1)).then_inc(wide_products, 1)

            pe.wait_ge(made, 2)
            pe.wait_ge(const_in, 16 * 8)
            nc.tensor.transpose(psum[:, Y, 0:P], w_nat[:, 0], identity[:])
            nc.tensor.transpose(psum[:, Y, P:2 * P], w_nat[:, 1], identity[:])
            nc.tensor.transpose(psum[:, Y, 2 * P:2 * P + BLOCKS], beta_rows, identity[0:BLOCKS, 0:BLOCKS])\
                .then_inc(setup_pe, 1)
            pe.wait_ge(setup_dve, 5)

            superblock(0, 0, 0, None)
            with pe.Fori(1, SUPERS) as s:
                superblock(0, 0, s, (0, s - 1))
            last_products(0)
            for b in range(BLOCKS):
                wide_block(0, b)
                if b == 3:
                    project(0, SUPERS - 1)
            with pe.Fori(1, WIDES) as q:
                for b in range(BLOCKS):
                    wide_block(q, b)
                    if b == 2:
                        turn_back(q - 1)
            for layer, pending in ((2, (1, None)), (3, (2, SUPERS - 1))):
                superblock(layer, 0, 0, pending)
                for quarter in range(QUARTERS):
                    with pe.Fori(max(quarter * QUARTER, 1), (quarter + 1) * QUARTER) as s:
                        superblock(layer, quarter, s, (layer, s - 1))
                last_products(layer)
            project(3, SUPERS - 1)

        def wide_count(k, q):
            return (q * (BLOCKS // 2 // RING) + (LOADS[1] + k) // RING + 1) * 16

        def pool_sums(s, g):
            return s * (2 * GROUPS - 1) + 2 * g - 1

        def wide_tile(n, b, h):
            at = (b % 2) * WIDE + h * 512
            return ring[:, n % RING].rearrange("p r c -> p (r c)")[:, at:at + 512]

        @block.scalar
        def _(act):
            def high_part(layer, quarter, s, c):
                i, g = c % BANKS, c // PER_CHUNK
                slot = (LOADS[layer] + g) % RING
                if loaded(layer, quarter, c):
                    if c % PER_CHUNK == 0:
                        act.wait_ge(arrived[slot], slot_count(layer, quarter, g, s))
                else:
                    act.wait_ge(transposed, turned_tiles(layer, quarter, s, c) + 1)
                if keeps(layer, quarter, order(layer, quarter)[g]):
                    before = kept_tiles(layer, quarter, s, g)
                    if not (isinstance(before, int) and before == 0):
                        act.wait_ge(kept_out[i], before // BANKS * 16)
                    nc.scalar.activation(kept[:, i], psum[:, i], ACT.Copy).then_inc(kept_ready, 1)
                if layer == 2 and first(s) and c < BANKS:
                    act.wait_ge(wide_products, WIDES * WIDE_TILES)
                elif layer != 0 or c >= BANKS or not first(s):
                    act.wait_ge(products, tiles(layer, quarter, s) + c - BANKS + 1)
                tile = ring[:, slot, c % PER_CHUNK] if loaded(layer, quarter, c) else psum[:, i]
                sums = {"accum_out": col_parts[:, c, bass.ds(s, 1)]} if layer == 0 else {}
                nc.scalar.activation(parts[:, i, 0], tile, ACT.Copy, **sums).then_inc(high_ready, 1)

            def copy_half(layer, quarter, s):
                act.wait_ge(products, tiles(layer, quarter, s) + len(order(layer, quarter)) * PER_CHUNK // 2)
                if layer != 0 or not first(s):
                    act.wait_ge(y_ready, unit(layer, s))
                nc.scalar.activation(acc_sb[:, 0:SUPER], psum[:, ACC], ACT.Copy).then_inc(half_copied, 1)

            def copy_early(quarter, s):
                act.wait_ge(products, tiles(2, quarter, s) + BLOCKS - PER_CHUNK)
                if not isinstance(s, int):
                    act.wait_ge(early_out, 16 * (s - QUARTER))
                nc.scalar.activation(early_sums, psum[:, EARLY], ACT.Copy).then_inc(early_copied, 1)

            def root(layer, t):
                act.wait_ge(var_ready, unit(layer, t) + 1)
                nc.scalar.activation(sd[:], var[:], ACT.Sqrt).then_inc(sd_ready, 1)

            def split(layer, t):
                if layer == 1:
                    act.wait_ge(scaled_ready, t + 1)
                else:
                    act.wait_ge(new_ready, unit(layer, t) + 1)
                nc.scalar.activation(x_high[(layer + 1) % 2][:, bass.ds(t * BLOCK_ROWS, BLOCK_ROWS), :],
                                     (u01 if layer == 1 else x_new[:]), ACT.Copy).then_inc(split_high, 1)

            def close(block, pending, wide, quarter=0):
                for layer, t, _, _, (stage, _) in stages(block - 1, pending, wide, quarter):
                    if stage == VARIANCE:
                        root(layer, t)
                    if stage == TIMES_D and layer != 3:
                        split(layer, t)

            def superblock(layer, quarter, s, pending):
                n = len(order(layer, quarter)) * PER_CHUNK
                for c in range(n):
                    high_part(layer, quarter, s, c)
                    if c == half_at(n) and not (layer == 3 and quarter > 0):
                        copy_half(layer, quarter, s)
                    close(c, pending, False, quarter)
                if layer == 2 and quarter > 0:
                    copy_early(quarter, s)
                close(n, pending, False, quarter)

            def wide_high_parts(q, b):
                n = LOADS[1] + b // 2
                if b % 2 == 0:
                    act.wait_ge(arrived[n % RING], wide_count(b // 2, q))
                for h in range(HALVES):
                    tile = b * HALVES + h
                    if tile < BANKS and isinstance(q, int):
                        act.wait_ge(products, SUPERS * BLOCKS)
                    else:
                        act.wait_ge(wide_products, q * WIDE_TILES + tile - BANKS + 1)
                    nc.scalar.activation(parts[:, tile % BANKS, 0], wide_tile(n, b, h), ACT.Copy)\
                        .then_inc(wide_high, 1)

            def copy_wide(q):
                act.wait_ge(wide_products, (q + 1) * WIDE_TILES)
                act.wait_ge(y_ready, unit(1, 2 * q))
                for h in range(HALVES):
                    last = nc.scalar.activation(acc_sb[:, h * 512:(h + 1) * 512], psum[:, h], ACT.Copy)
                last.then_inc(wide_copied, 1)

            act.wait_ge(const_in, 16 * 8)
            for q in range(RING):
                act.wait_ge(arrived[q], 16)
                to = x_high[0][:, q * (BLOCKS // RING):(q + 1) * (BLOCKS // RING)].rearrange("p b f -> p (b f)")
                nc.scalar.activation(to, x0_quarter(q).rearrange("p b f -> p (b f)"), ACT.Identity, scale=a_bc[:])\
                    .then_inc(x0_high_ready, 1)

            superblock(0, 0, 0, None)
            with act.Fori(1, SUPERS) as s:
                superblock(0, 0, s, (0, s - 1, None))
            for b in range(BLOCKS):
                wide_high_parts(0, b)
                close(b, (0, SUPERS - 1, None), True)
                if b == FACTORS_AT + 2:
                    act.wait_ge(factors, 7)
                    nc.scalar.activation(small[:, 1], small[:, 0], ACT.Sqrt).then_inc(factor_root, 1)
            with act.Fori(1, WIDES) as q:
                for b in range(BLOCKS):
                    wide_high_parts(q, b)
                    if b == 0:
                        copy_wide(q - 1)
                    close(b, (1, 2 * q - 2, None), True)
            copy_wide(WIDES - 1)
            for layer, pending in ((2, (1, SUPERS - 2, None)), (3, (2, SUPERS - 1, None))):
                superblock(layer, 0, 0, pending)
                for quarter in range(QUARTERS):
                    start = max(quarter * QUARTER, 1)
                    if layer == 2 and quarter == 1:
                        superblock(layer, quarter, start, (layer, start - 1, None))
                        start += 1
                    with act.Fori(start, (quarter + 1) * QUARTER) as s:
                        superblock(layer, quarter, s, (layer, s - 1, None))
            root(3, SUPERS - 1)

        @block.vector
        def _(dve):
            def low_part(layer, quarter, s, c):
                i, slot = c % BANKS, (LOADS[layer] + c // PER_CHUNK) % RING
                dve.wait_ge(high_ready, tiles(layer, quarter, s) + c + 1)
                tile = ring[:, slot, c % PER_CHUNK] if loaded(layer, quarter, c) else psum[:, i]
                nc.vector.tensor_tensor(parts[:, i, 1], tile, parts[:, i, 0].bitcast(F32), ALU.subtract)\
                    .then_inc(low_ready, 1)

            def row_sums(s, g):
                n = LOADS[0] + g
                dve.wait_ge(arrived[n % RING], slot_count(0, 0, g, s))
                dve.wait_ge(rows_pool, pool_sums(s, g + 1))
                nc.vector.tensor_reduce(row_parts[:, g, bass.ds(s, 1)], ring[:, n % RING, 0], AX.X, ALU.add)\
                    .then_inc(rows_dve, 1)

            def rows(tensor, t):
                return tensor[:, bass.ds(t * BLOCK_ROWS, BLOCK_ROWS)]

            def unit_row_sums(t, block):
                if block == 0:
                    dve.wait_ge(rows_dve, (t + 1) * GROUPS)
                    nc.vector.tensor_reduce(row_sum[:, bass.ds(t * BLOCK_ROWS, 1)],
                                            row_parts[:, :, bass.ds(t, 1)].rearrange("p g a -> p (g a)"),
                                            AX.X, ALU.add)
                    dve.wait_ge(rows_pool, pool_sums(t, GROUPS))
                    nc.vector.tensor_reduce(row_sum[:, bass.ds(t * BLOCK_ROWS + 1, 1)], row_acc[:, 0], AX.X,
                                            ALU.add)
                if block == 1:
                    nc.vector.tensor_reduce(row_sum[:, bass.ds(t * BLOCK_ROWS + 2, 2)], row_acc[:, 1:3], AX.X,
                                            ALU.add).then_inc(rows_done, 1)

            def add_early(quarter, s):
                dve.wait_ge(products, tiles(3, quarter, s) + len(order(3, quarter)) * PER_CHUNK // 2)
                dve.wait_ge(early_in, 16 * (s - QUARTER + 1))
                dve.wait_ge(y_ready, unit(3, s))
                nc.vector.tensor_tensor(acc_sb[:, 0:SUPER], psum[:, ACC], kept[:, EARLY_IN], ALU.add)\
                    .then_inc(half_copied, 1)

            def sum_halves(layer, t, all_tiles, half):
                if half == 0:
                    dve.wait_ge(half_copied, turned(layer, t) + 1)
                    dve.wait_ge(products, all_tiles)
                span = slice(half * SUPER // 2, (half + 1) * SUPER // 2)
                nc.vector.tensor_tensor(acc_sb[:, span], acc_sb[:, span], psum[:, ACC2, span], ALU.add)\
                    .then_inc(acc_copied, 1)

            def degree(t, second):
                def after(k):
                    dve.wait_ge(deg_steps, t * DEG_STEPS + k)

                if not second:
                    dve.wait_ge(rows_done, t + 1)
                    nc.vector.tensor_scalar(deg[:, 0], rows(row_sum, t), a_bc[:], one_minus_a[:], ALU.mult, ALU.add)\
                        .then_inc(deg_steps, 1)
                    after(1)
                    nc.vector.tensor_scalar(deg[:, 1], deg[:, 0], 0.0, None, ALU.is_equal).then_inc(deg_steps, 1)
                    after(2)
                    nc.vector.tensor_tensor(deg[:, 2], deg[:, 0], deg[:, 1], ALU.add).then_inc(deg_steps, 1)
                    return
                after(3)
                nc.vector.reciprocal(deg[:, 0], deg[:, 2]).then_inc(deg_steps, 1)
                nc.vector.tensor_scalar(deg[:, 4], deg[:, 1], -1.0, 1.0, ALU.mult, ALU.add).then_inc(deg_steps, 1)
                after(5)
                nc.vector.tensor_tensor(deg[:, 3], deg[:, 0], deg[:, 4], ALU.mult).then_inc(deg_steps, 1)

            def scale(layer, t, parity, pair, r):
                by = (deg[:, 3] if layer == 0 else
                      rows({1: col_factor, 2: d_half, 3: degree3}[layer], t))
                if r == 0:
                    dve.wait_ge(y_ready, unit(layer, t) + 1)
                    if layer == 0:
                        dve.wait_ge(deg_steps, (t + 1) * DEG_STEPS)
                    if layer == 2 and isinstance(t, int) and t == 0:
                        dve.wait_ge(split_done, unit(2, 0))
                    if layer == 1:
                        wait_for_x(dve, 1, t)
                        dve.wait_ge(split_done, unit(1, t))
                plus = x_res[parity][:, r] if layer == 1 else bias[:, {0: 0, 2: 1, 3: 2}[layer]]
                u = u01 if layer < 2 else u23
                last = nc.vector.scalar_tensor_tensor(u[:, r, :], psum[:, Y + parity, r * P:(r + 1) * P],
                                                      by[:, r:r + 1], plus, ALU.mult, ALU.add)
                if r == BLOCK_ROWS - 1:
                    last.then_inc(y_used, 1)

            def residual(layer, t):
                u = u01 if layer < 2 else u23
                dve.wait_ge(y_used, unit(layer, t) + 1)
                wait_for_x(dve, layer, t)
                if layer == 0:
                    done = nc.vector.scalar_tensor_tensor(u, u, 0.0, x_res[0][:], ALU.max, ALU.add)
                else:
                    done = nc.vector.tensor_tensor(u, u, x_res[0][:], ALU.add)
                done.then_inc(res_used, 1)

            def close(block, pending, wide, quarter=0):
                for layer, t, parity, pair, step in stages(block, pending, wide, quarter):
                    close_step(layer, t, parity, pair, *step)

            def close_step(layer, t, parity, pair, stage, r):
                u = u01 if layer < 2 else u23
                n = unit(layer, t)
                if stage == DEGREE and layer == 0:
                    degree(t, False)
                if stage == DEGREE2 and layer == 0:
                    degree(t, True)
                if stage == SCALE:
                    scale(layer, t, parity, pair, r)
                if stage == RESIDUAL and layer != 1:
                    residual(layer, t)
                if stage == STATS:
                    if r == 0:
                        if layer == 1:
                            dve.wait_ge(y_used, n + 1)
                        else:
                            dve.wait_ge(res_used, turned(layer, t) + 1)
                    nc.vector.bn_stats(stats[:, 2 * r], u[:, 2 * r, :])
                    last = nc.vector.bn_stats(stats[:, 2 * r + 1], u[:, 2 * r + 1, :])
                    if r == 1:
                        last.then_inc(stats_ready, 1)
                if stage == MOMENTS:
                    dve.wait_ge(stats_ready, n + 1)
                    nc.vector.tensor_copy(rt[:, 0], stats[:, :, 0])
                    for b in range(BLOCK_ROWS):
                        last = nc.vector.bn_aggr(moments[:, b], stats[:, b])
                    last.then_inc(moments_ready, 1)
                if stage == VARIANCE:
                    dve.wait_ge(moments_ready, n + 1)
                    nc.vector.tensor_scalar(var[:], moments[:, :, 1], EPS, None, ALU.add).then_inc(var_ready, 1)
                if stage == ROOT:
                    dve.wait_ge(sd_ready, n + 1)
                    nc.vector.reciprocal(rs[:], sd[:]).then_inc(root_steps, 1)
                    dve.wait_ge(root_steps, n * ROOT_STEPS + 1)
                    nc.vector.tensor_tensor(rt[:, 0], var[:], rs[:], ALU.mult).then_inc(root_steps, 1)
                    dve.wait_ge(root_steps, n * ROOT_STEPS + 2)
                    nc.vector.tensor_tensor(rt[:, 1], rt[:, 0], rs[:], ALU.mult).then_inc(root_steps, 1)
                if stage == ROOT2:
                    dve.wait_ge(root_steps, n * ROOT_STEPS + 3)
                    nc.vector.tensor_scalar(rt[:, 2], rt[:, 1], -0.5, 1.5, ALU.mult, ALU.add)\
                        .then_inc(root_steps, 1)
                    dve.wait_ge(root_steps, n * ROOT_STEPS + 4)
                    nc.vector.tensor_tensor(rt[:, 3], rt[:, 2], rs[:], ALU.mult).then_inc(root_steps, 1)
                if stage == NORM:
                    if r == 0:
                        dve.wait_ge(root_steps, (n + 1) * ROOT_STEPS)
                        if not (layer == 0 and isinstance(t, int) and t == 0):
                            dve.wait_ge(split_done, min_split(layer, t))
                        if layer == 1 and not first(t) or layer == 3:
                            dve.wait_ge(stored, 16 * (t if layer == 1 else SUPERS + t))
                        if layer == 2 and first(t):
                            dve.wait_ge(stored, 16 * SUPERS)
                    last = nc.vector.tensor_scalar(x_new[:, r], u[:, r, :], moments[:, r, 0:1],
                                                   rt[:, 3, r:r + 1], ALU.subtract, ALU.mult)
                    if r == BLOCK_ROWS - 1:
                        last.then_inc(new_ready, 1)
                if stage == TIMES_D and layer == 1:
                    dve.wait_ge(new_ready, n + 1)
                    by = rows(d_half, t)
                    for b in range(BLOCK_ROWS):
                        last = nc.vector.tensor_scalar(u[:, b, :], x_new[:, b], by[:, b:b + 1], None,
                                                       ALU.mult)
                    last.then_inc(scaled_ready, 1)
                if stage == LOW and layer != 3:
                    dve.wait_ge(split_high, n + 1)
                    span = bass.ds(t * BLOCK_ROWS, BLOCK_ROWS)
                    nc.vector.tensor_tensor(x_low[(layer + 1) % 2][:, span, :],
                                            (u if layer == 1 else x_new[:]),
                                            x_high[(layer + 1) % 2][:, span, :].bitcast(F32), ALU.subtract)\
                        .then_inc(split_done, 1)

            def min_split(layer, t):
                return unit(3, 0) if layer == 3 else unit(layer, t)

            def diagonal(quarter, s):
                dve.wait_ge(products, tiles(3, quarter, s))
                for r in range(BLOCK_ROWS):
                    last = nc.vector.tensor_scalar(diag[:, r], identity[:],
                                                   rows(beta_col, s)[:, r:r + 1], None, ALU.mult)
                last.then_inc(diag_ready, 1)

            def superblock(layer, quarter, s, pending):
                n = len(order(layer, quarter)) * PER_CHUNK
                for c in range(n):
                    low_part(layer, quarter, s, c)
                    if layer == 0 and pending:
                        unit_row_sums(pending[1], c)
                    if pending and pending[0] != 1 and c in SUM_AT:
                        sum_halves(*pending[:2], tiles(layer, quarter, s), SUM_AT.index(c))
                    if layer == 0 and c % PER_CHUNK == PER_CHUNK - 1:
                        row_sums(s, c // PER_CHUNK)
                    if layer == 3 and c == max(n - 16, LAG + 2):
                        diagonal(quarter, s)
                    if c == half_at(n) and layer == 3 and quarter > 0:
                        add_early(quarter, s)
                    close(c, pending, False, quarter)

            def wide_low_parts(q, b):
                for h in range(HALVES):
                    tile = b * HALVES + h
                    i = tile % BANKS
                    dve.wait_ge(wide_high, q * WIDE_TILES + tile + 1)
                    nc.vector.tensor_tensor(parts[:, i, 1], wide_tile(LOADS[1] + b // 2, b, h),
                                            parts[:, i, 0].bitcast(F32), ALU.subtract).then_inc(wide_low, 1)

            def layer_factors(part):
                def after(k):
                    dve.wait_ge(factors, k)

                if part == 0:
                    nc.vector.tensor_reduce(col_sum[:], col_parts[:], AX.X, ALU.add).then_inc(factors, 1)
                    after(1)
                    nc.vector.tensor_scalar(small[:, 2], col_sum[:], 0.0, None, ALU.is_equal).then_inc(factors, 1)
                    after(2)
                    nc.vector.tensor_tensor(small[:, 3], col_sum[:], small[:, 2], ALU.add).then_inc(factors, 1)
                    after(3)
                    nc.vector.reciprocal(small[:, 4], small[:, 3]).then_inc(factors, 1)
                    nc.vector.tensor_scalar(small[:, 5], small[:, 2], -1.0, 1.0, ALU.mult, ALU.add)\
                        .then_inc(factors, 1)
                    after(5)
                    nc.vector.tensor_tensor(col_factor[:], small[:, 4], small[:, 5], ALU.mult).then_inc(factors, 1)
                    nc.vector.tensor_scalar(small[:, 0], row_sum[:], 1e-8, None, ALU.add).then_inc(factors, 1)
                if part == 1:
                    nc.vector.tensor_tensor(small[:, 6], row_sum[:], beta_col[:], ALU.add).then_inc(factors, 1)
                    after(8)
                    nc.vector.reciprocal(degree3[:], small[:, 6]).then_inc(factors, 1)
                    dve.wait_ge(factor_root, 1)
                    nc.vector.reciprocal(small[:, 7], small[:, 1]).then_inc(factors, 1)
                    after(10)
                    nc.vector.tensor_tensor(small[:, 8], small[:, 0], small[:, 7], ALU.mult).then_inc(factors, 1)
                    after(11)
                    nc.vector.tensor_tensor(small[:, 9], small[:, 8], small[:, 7], ALU.mult).then_inc(factors, 1)
                    after(12)
                    nc.vector.tensor_scalar(small[:, 10], small[:, 9], -0.5, 1.5, ALU.mult, ALU.add)\
                        .then_inc(factors, 1)
                    after(13)
                    nc.vector.tensor_tensor(d_half[:], small[:, 10], small[:, 7], ALU.mult).then_inc(factors, 1)
                    after(14)

            dve.wait_ge(const_in, 16 * 8)
            nc.vector.tensor_scalar(one_minus_a[:], a_bc[:], -1.0, 1.0, ALU.mult, ALU.add).then_inc(setup_dve, 1)
            dve.wait_ge(setup_dve, 1)
            dve.wait_ge(made, 2)
            nc.vector.tensor_scalar(diag0[:], identity[:], one_minus_a[:], None, ALU.mult).then_inc(setup_dve, 1)
            dve.wait_ge(setup_pe, 1)
            for i in range(2):
                nc.vector.tensor_copy(w_mov[:, i], psum[:, Y, i * P:(i + 1) * P]).then_inc(setup_dve, 1)
            nc.vector.tensor_copy(beta_col[:], psum[:, Y, 2 * P:2 * P + BLOCKS]).then_inc(setup_dve, 1)
            dve.wait_ge(setup_dve, 5)
            for q in range(RING):
                span = slice(q * (BLOCKS // RING), (q + 1) * (BLOCKS // RING))
                dve.wait_ge(x0_high_ready, q + 1)
                nc.vector.scalar_tensor_tensor(x_low[0][:, span].rearrange("p b f -> p (b f)"),
                                               x0_quarter(q).rearrange("p b f -> p (b f)"), a_bc[:],
                                               x_high[0][:, span].rearrange("p b f -> p (b f)").bitcast(F32),
                                               ALU.mult, ALU.subtract).then_inc(x0_ready, 1)

            superblock(0, 0, 0, None)
            with dve.Fori(1, SUPERS) as s:
                superblock(0, 0, s, (0, s - 1, None))
            for b in range(BLOCKS):
                wide_low_parts(0, b)
                unit_row_sums(SUPERS - 1, b)
                if b < 2:
                    sum_halves(0, SUPERS - 1, SUPERS * BLOCKS, b)
                close(b, (0, SUPERS - 1, None), True)
                if b == FACTORS_AT:
                    layer_factors(0)
                if b == FACTORS_AT + 4:
                    layer_factors(1)
            with dve.Fori(1, WIDES) as q:
                for b in range(BLOCKS):
                    wide_low_parts(q, b)
                    close(b, (1, 2 * q - 2, q - 1), True)
            for layer, pending in ((2, (1, SUPERS - 2, WIDES - 1)), (3, (2, SUPERS - 1, None))):
                superblock(layer, 0, 0, pending)
                for quarter in range(QUARTERS):
                    with dve.Fori(max(quarter * QUARTER, 1), (quarter + 1) * QUARTER) as s:
                        superblock(layer, quarter, s, (layer, s - 1, None))
            for half in range(2):
                sum_halves(3, SUPERS - 1, tiles(3, QUARTERS - 1, SUPERS), half)
            for step in STEPS:
                close_step(3, SUPERS - 1, 0, None, *step)

        @block.gpsimd
        def _(pool):
            nc.gpsimd.memset(identity[:], 0.0).then_inc(made, 1)
            pool.wait_ge(made, 1)
            nc.gpsimd.affine_select(out=identity[:], in_=identity[:], compare_op=ALU.not_equal, fill=1.0, base=0,
                                    pattern=[[-1, P]], channel_multiplier=1).then_inc(made, 1)

            def row_sums(s):
                for g in range(GROUPS):
                    slot = (LOADS[0] + g) % RING
                    halves = [ring[:, slot, 1:4, h * (CHUNK // 2):(h + 1) * (CHUNK // 2)] for h in range(2)]
                    pool.wait_ge(arrived[slot], slot_count(0, 0, g, s))
                    if g == 0:
                        if not isinstance(s, int):
                            pool.wait_ge(rows_done, s)
                        nc.gpsimd.tensor_tensor(row_acc[:], halves[0], halves[1], ALU.add).then_inc(rows_pool, 1)
                        continue
                    for h in range(2):
                        pool.wait_ge(rows_pool, pool_sums(s, g) + h)
                        nc.gpsimd.tensor_tensor(row_acc[:], row_acc[:], halves[h], ALU.add).then_inc(rows_pool, 1)

            row_sums(0)
            with pool.Fori(1, SUPERS) as s:
                row_sums(s)
            def make_x(parity, t):
                span = bass.ds(t * BLOCK_ROWS, BLOCK_ROWS)
                nc.gpsimd.tensor_tensor(x_res[parity][:], x_high[1][:, span, :].bitcast(F32),
                                        x_low[1][:, span, :].bitcast(F32), ALU.add).then_inc(res_made, 1)

            pool.wait_ge(res_used, SUPERS)
            pool.wait_ge(split_done, SUPERS)
            for parity in range(2):
                make_x(parity, parity)
            with pool.Fori(1, WIDES) as q:
                for parity in range(2):
                    pool.wait_ge(y_used, unit(1, 2 * q - 1 + parity))
                    make_x(parity, 2 * q + parity)
            with pool.Fori(QUARTER, SUPERS) as s:
                pool.wait_ge(early_copied, s - QUARTER + 1)
                pool.dma_start(early[s], early_sums).then_inc(early_out, 16)
            pool.wait_ge(split_done, unit(3, 0))
            with pool.Fori(0, QUARTER) as s:
                pool.wait_ge(res_used, turned(3, s))
                make_x(0, s)
            pool.wait_ge(early_out, 16 * (SUPERS - QUARTER))
            pool.wait_ge(kept_out[EARLY_IN], 16 * (kept_in_all() // BANKS))
            with pool.Fori(QUARTER, SUPERS) as s:
                pool.wait_ge(half_copied, turned(3, s))
                pool.dma_start(kept[:, EARLY_IN], early[s]).then_inc(early_in, 16)
                pool.wait_ge(res_used, turned(3, s))
                make_x(0, s)


_ARGS = ["x", "adj", "L0_gnn_alpha", "L0_gnn_W", "L0_gnn_b", "L2_gnn_W", "L2_gnn_b", "L3_gnn_kernel",
         "L3_gnn_bias", "L3_gnn_beta"]


def kernel(x, adj, L0_gnn_t, L0_gnn_alpha, L0_gnn_W, L0_gnn_b, L2_gnn_W, L2_gnn_b, L3_gnn_kernel,
           L3_gnn_bias, L3_gnn_beta):
    import numpy as np
    import concourse.bacc as bacc
    from concourse.bass_utils import run_bass_kernel_spmd

    given = [x, adj, L0_gnn_alpha, L0_gnn_W, L0_gnn_b, L2_gnn_W, L2_gnn_b, L3_gnn_kernel, L3_gnn_bias,
             L3_gnn_beta]
    nc = bacc.Bacc("TRN2", target_bir_lowering=False, num_devices=1)
    arrays, args = {}, []
    for name, value in zip(_ARGS, given):
        a = np.ascontiguousarray(value)
        arrays[f"in_{name}"] = a
        args.append(nc.dram_tensor(f"in_{name}", a.shape, mybir.dt.from_np(a.dtype), kind="ExternalInput").ap())
    out = nc.dram_tensor("out", x.shape, mybir.dt.float32, kind="ExternalOutput").ap()
    plain = nc.dram_tensor("x2_plain", x.shape, mybir.dt.float32, kind="Internal").ap()
    rows, per_load = 512, 4
    turned = nc.dram_tensor("a_turned", (x.shape[0] // rows, x.shape[0] // rows, P, per_load, rows),
                            mybir.dt.float32, kind="Internal").ap()
    early = nc.dram_tensor("early", (x.shape[0] // rows, P, rows), mybir.dt.float32, kind="Internal").ap()
    build(nc, *args, out, plain, turned, early)
    return run_bass_kernel_spmd(nc, [arrays], core_ids=[0]).results[0]["out"]
```
